# Optimizing a Trainium2 kernel written in Bass

```python
import numpy as np
import jax
import jax.numpy as jnp

def _softmax(x, axis=-1):
    return jax.nn.softmax(x, axis=axis)

def _gelu(x):
    return jax.nn.gelu(x, approximate=True)

def _silu(x):
    return jax.nn.silu(x)

def _sigmoid(x):
    return jax.nn.sigmoid(x)

def _layernorm(x, axis=-1, eps=1e-05):
    m = jnp.mean(x, axis=axis, keepdims=True)
    v = jnp.var(x, axis=axis, keepdims=True)
    return (x - m) / jnp.sqrt(v + eps)

def _scatter_add(tgt, idx, src, axis=0):
    return tgt.at[idx].add(src)

def _segment_sum(src, seg, n):
    return jax.ops.segment_sum(src, seg, n)
kernel_name = 'mk_hybrid_d1_jaxref_r8_6499fb'

def setup_inputs(seed: int=0):
    np.random.seed(seed)
    _w = jnp.asarray

    def _L0_attn_a_setup():
        import jax, jax.numpy as jnp
        import numpy as np
        import math
        D_MODEL = 128
        N_HEADS = 16
        HEAD_DIM = D_MODEL // N_HEADS
        ROT_DIM = min(32, D_MODEL // 4)

        def _xavier(key, fan_in, fan_out):
            lim = math.sqrt(6.0 / (fan_in + fan_out))
            return jax.random.uniform(key, (fan_in, fan_out), jnp.float32, -lim, lim)
        key = jax.random.key(seed)
        ks = jax.random.split(key, 6)
        x = jax.random.normal(ks[0], (2, 256, D_MODEL), jnp.float32)
        Wq = _xavier(ks[1], D_MODEL, D_MODEL)
        Wk = _xavier(ks[2], D_MODEL, D_MODEL)
        Wv = _xavier(ks[3], D_MODEL, D_MODEL)
        Wr = _xavier(ks[4], D_MODEL, N_HEADS * ROT_DIM)
        Wo = _xavier(ks[5], D_MODEL, D_MODEL)
        z = jnp.zeros((D_MODEL,), jnp.float32)
        zr = jnp.zeros((N_HEADS * ROT_DIM,), jnp.float32)
        return {'x': x, 'Wq': Wq, 'bq': z, 'Wk': Wk, 'bk': z, 'Wv': Wv, 'bv': z, 'Wr': Wr, 'br': zr, 'Wo': Wo, 'bo': z}
    _L0_attn_a_in = _L0_attn_a_setup()

    def _L0_attn_b_setup():
        import jax, jax.numpy as jnp
        import numpy as np
        NUM_HEADS = 16
        DEPTH = 0

        def rotate_half(x):
            x1, x2 = jnp.split(x, 2, axis=-1)
            return jnp.concatenate((-x2, x1), axis=-1)

        def rotary_tables(seq_len, rot_dim, dtype):
            inv_freq = 1.0 / 10000.0 ** (jnp.arange(0, rot_dim, 2, dtype=jnp.float32) / rot_dim)
            freqs = jnp.arange(seq_len, dtype=jnp.float32)[:, None] * inv_freq[None, :]
            emb = jnp.concatenate((freqs, freqs), axis=-1)
            return (emb.astype(dtype), jnp.cos(emb).astype(dtype), jnp.sin(emb).astype(dtype))
        key = jax.random.key(seed)
        ks = jax.random.split(key, 7)
        B, N, C = (1, 256, 128)
        hd = C // NUM_HEADS
        std_qkv = (1.0 / C) ** 0.5
        std_proj = (1.0 / (2 * C)) ** 0.5
        return {'x': jax.random.normal(ks[0], (B, N, C), dtype=jnp.float32), 'W_qkv': jax.random.normal(ks[1], (6 * C, C), dtype=jnp.float32) * std_qkv, 'W_proj': jax.random.normal(ks[2], (C, 2 * C), dtype=jnp.float32) * std_proj, 'lambda_q1': jax.random.normal(ks[3], (hd,), dtype=jnp.float32) * 0.1, 'lambda_q2': jax.random.normal(ks[4], (hd,), dtype=jnp.float32) * 0.1, 'lambda_k1': jax.random.normal(ks[5], (hd,), dtype=jnp.float32) * 0.1, 'lambda_k2': jax.random.normal(ks[6], (hd,), dtype=jnp.float32) * 0.1}
    _L0_attn_b_in = _L0_attn_b_setup()

    def _L0_ffn_setup():
        import jax, jax.numpy as jnp
        import numpy as np
        D_MODEL = 128
        D_HIDDEN = 512
        NUM_EXPERTS = 8
        B, T = (2, 256)
        key = jax.random.key(seed)
        ks = jax.random.split(key, 8)
        s = 0.02
        x = jax.random.normal(ks[0], (B, T, D_MODEL), dtype=jnp.float32)
        Wg = jax.random.normal(ks[1], (D_MODEL, NUM_EXPERTS), dtype=jnp.float32) * s
        bg = jnp.zeros((NUM_EXPERTS,), dtype=jnp.float32)
        W1 = jax.random.normal(ks[2], (NUM_EXPERTS, D_MODEL, D_HIDDEN), dtype=jnp.float32) * s
        b1 = jnp.zeros((NUM_EXPERTS, D_HIDDEN), dtype=jnp.float32)
        W2 = jax.random.normal(ks[3], (NUM_EXPERTS, D_HIDDEN, D_MODEL), dtype=jnp.float32) * s
        b2 = jnp.zeros((NUM_EXPERTS, D_MODEL), dtype=jnp.float32)
        return {'x': x, 'Wg': Wg, 'bg': bg, 'W1': W1, 'b1': b1, 'W2': W2, 'b2': b2}
    _L0_ffn_in = _L0_ffn_setup()
    _d = {'L0_attn_a_x': _L0_attn_a_in['x'], 'L0_attn_a_Wq': _L0_attn_a_in['Wq'], 'L0_attn_a_bq': _L0_attn_a_in['bq'], 'L0_attn_a_Wk': _L0_attn_a_in['Wk'], 'L0_attn_a_bk': _L0_attn_a_in['bk'], 'L0_attn_a_Wv': _L0_attn_a_in['Wv'], 'L0_attn_a_bv': _L0_attn_a_in['bv'], 'L0_attn_a_Wr': _L0_attn_a_in['Wr'], 'L0_attn_a_br': _L0_attn_a_in['br'], 'L0_attn_a_Wo': _L0_attn_a_in['Wo'], 'L0_attn_a_bo': _L0_attn_a_in['bo'], 'L0_attn_b_W_qkv': _L0_attn_b_in['W_qkv'], 'L0_attn_b_W_proj': _L0_attn_b_in['W_proj'], 'L0_attn_b_lambda_q1': _L0_attn_b_in['lambda_q1'], 'L0_attn_b_lambda_q2': _L0_attn_b_in['lambda_q2'], 'L0_attn_b_lambda_k1': _L0_attn_b_in['lambda_k1'], 'L0_attn_b_lambda_k2': _L0_attn_b_in['lambda_k2'], 'L0_ffn_Wg': _L0_ffn_in['Wg'], 'L0_ffn_bg': _L0_ffn_in['bg'], 'L0_ffn_W1': _L0_ffn_in['W1'], 'L0_ffn_b1': _L0_ffn_in['b1'], 'L0_ffn_W2': _L0_ffn_in['W2'], 'L0_ffn_b2': _L0_ffn_in['b2']}
    _x0 = _d['L0_attn_a_x']
    _d['L0_attn_a_x'] = jax.random.normal(jax.random.fold_in(jax.random.key(seed), 1), (8, 512, 128), dtype=_x0.dtype)
    del _x0
    return _d

def reference(L0_attn_a_x, L0_attn_a_Wq, L0_attn_a_bq, L0_attn_a_Wk, L0_attn_a_bk, L0_attn_a_Wv, L0_attn_a_bv, L0_attn_a_Wr, L0_attn_a_br, L0_attn_a_Wo, L0_attn_a_bo, L0_attn_b_W_qkv, L0_attn_b_W_proj, L0_attn_b_lambda_q1, L0_attn_b_lambda_q2, L0_attn_b_lambda_k1, L0_attn_b_lambda_k2, L0_ffn_Wg, L0_ffn_bg, L0_ffn_W1, L0_ffn_b1, L0_ffn_W2, L0_ffn_b2):

    def _L0_attn_a_ref(x, Wq, bq, Wk, bk, Wv, bv, Wr, br, Wo, bo):
        import jax, jax.numpy as jnp
        import numpy as np
        import math
        D_MODEL = 128
        N_HEADS = 16
        HEAD_DIM = D_MODEL // N_HEADS
        ROT_DIM = min(32, D_MODEL // 4)

        def _xavier(key, fan_in, fan_out):
            lim = math.sqrt(6.0 / (fan_in + fan_out))
            return jax.random.uniform(key, (fan_in, fan_out), jnp.float32, -lim, lim)
        B, S, _ = x.shape
        H, Dh, Dr = (N_HEADS, HEAD_DIM, ROT_DIM)
        q = (x @ Wq + bq).reshape(B, S, H, Dh)
        k = (x @ Wk + bk).reshape(B, S, H, Dh)
        v = (x @ Wv + bv).reshape(B, S, H, Dh)
        r = (x @ Wr + br).reshape(B, S, H, Dr)
        q = jnp.concatenate([q, r], axis=-1)
        k = jnp.concatenate([k, r], axis=-1)
        scale = 1.0 / math.sqrt(Dh + Dr)
        scores = jnp.einsum('bqhd,bkhd->bhqk', q * scale, k)
        attn = jax.nn.softmax(scores, axis=-1)
        out = jnp.einsum('bhqk,bkhd->bqhd', attn, v).reshape(B, S, H * Dh)
        return out @ Wo + bo

    def _L0_attn_b_ref(x, W_qkv, W_proj, lambda_q1, lambda_q2, lambda_k1, lambda_k2):
        import jax, jax.numpy as jnp
        import numpy as np
        NUM_HEADS = 16
        DEPTH = 0

        def rotate_half(x):
            x1, x2 = jnp.split(x, 2, axis=-1)
            return jnp.concatenate((-x2, x1), axis=-1)

        def rotary_tables(seq_len, rot_dim, dtype):
            inv_freq = 1.0 / 10000.0 ** (jnp.arange(0, rot_dim, 2, dtype=jnp.float32) / rot_dim)
            freqs = jnp.arange(seq_len, dtype=jnp.float32)[:, None] * inv_freq[None, :]
            emb = jnp.concatenate((freqs, freqs), axis=-1)
            return (emb.astype(dtype), jnp.cos(emb).astype(dtype), jnp.sin(emb).astype(dtype))
        B, N, C = x.shape
        H = NUM_HEADS
        hd = C // H
        scale = hd ** (-0.5)
        lambda_init = 0.8 - 0.6 * np.exp(-0.3 * DEPTH)
        qkv = jnp.einsum('bnc,dc->bnd', x, W_qkv)
        qkv = qkv.reshape(B, N, 6, H, hd).transpose(2, 0, 3, 1, 4)
        q = jnp.concatenate((qkv[0], qkv[1]), axis=-1)
        k = jnp.concatenate((qkv[2], qkv[3]), axis=-1)
        v = jnp.concatenate((qkv[4], qkv[5]), axis=-1)
        _, cos, sin = rotary_tables(N, 2 * hd, x.dtype)
        q = q * cos + rotate_half(q) * sin
        k = k * cos + rotate_half(k) * sin
        q1, q2 = jnp.split(q, 2, axis=-1)
        k1, k2 = jnp.split(k, 2, axis=-1)
        attn1 = jnp.einsum('bhid,bhjd->bhij', q1, k1) * scale
        attn2 = jnp.einsum('bhid,bhjd->bhij', q2, k2) * scale
        lam1 = jnp.exp(jnp.sum(lambda_q1 * lambda_k1))
        lam2 = jnp.exp(jnp.sum(lambda_q2 * lambda_k2))
        lam = (lam1 - lam2 + lambda_init).astype(x.dtype)
        probs = jax.nn.softmax(attn1, axis=-1) - lam * jax.nn.softmax(attn2, axis=-1)
        out = jnp.einsum('bhij,bhjd->bhid', probs, v)
        out = out.transpose(0, 2, 1, 3).reshape(B, N, 2 * C)
        out = jnp.einsum('bnd,cd->bnc', out, W_proj)
        return out

    def _L0_ffn_ref(x, Wg, bg, W1, b1, W2, b2):
        import jax, jax.numpy as jnp
        import numpy as np
        D_MODEL = 128
        D_HIDDEN = 512
        NUM_EXPERTS = 8
        B, T = (2, 256)
        gate_logits = jnp.einsum('btd,de->bte', x, Wg) + bg
        gate_scores = jax.nn.softmax(gate_logits, axis=-1)
        top1_idx = jnp.argmax(gate_scores, axis=-1)
        top1_mask = jax.nn.one_hot(top1_idx, NUM_EXPERTS, dtype=x.dtype)
        top1_weight = jnp.sum(gate_scores * top1_mask, axis=-1, keepdims=True)
        h = jax.nn.silu(jnp.einsum('btd,edh->bteh', x, W1) + b1)
        o = jnp.einsum('bteh,ehd->bted', h, W2) + b2
        y = jnp.sum(o * top1_mask[..., None], axis=2) * top1_weight
        return y
    x = L0_attn_a_x
    x = x + _L0_attn_a_ref(_layernorm(x, axis=-1), L0_attn_a_Wq, L0_attn_a_bq, L0_attn_a_Wk, L0_attn_a_bk, L0_attn_a_Wv, L0_attn_a_bv, L0_attn_a_Wr, L0_attn_a_br, L0_attn_a_Wo, L0_attn_a_bo)
    x = x + _L0_ffn_ref(_layernorm(x, axis=-1), L0_ffn_Wg, L0_ffn_bg, L0_ffn_W1, L0_ffn_b1, L0_ffn_W2, L0_ffn_b2)
    x = x + _L0_attn_b_ref(_layernorm(x, axis=-1), L0_attn_b_W_qkv, L0_attn_b_W_proj, L0_attn_b_lambda_q1, L0_attn_b_lambda_q2, L0_attn_b_lambda_k1, L0_attn_b_lambda_k2)
    x = x + _L0_ffn_ref(_layernorm(x, axis=-1), L0_ffn_Wg, L0_ffn_bg, L0_ffn_W1, L0_ffn_b1, L0_ffn_W2, L0_ffn_b2)
    return x

_drawn_inputs = setup_inputs


def setup_inputs(seed=0):
    import zlib

    import numpy as np

    out = dict(_drawn_inputs(seed))
    spreads = {'L0_attn_a_bq': (0.0, 0.8),
     'L0_attn_a_bk': (0.0, 0.8),
     'L0_attn_a_bv': (0.0, 0.1),
     'L0_attn_a_br': (0.0, 0.8),
     'L0_attn_a_bo': (0.0, 0.1),
     'L0_ffn_bg': (0.0, 0.391),
     'L0_ffn_b1': (0.0, 0.8),
     'L0_ffn_b2': (0.0, 0.1)}
    factors = {'L0_attn_b_lambda_q1': 8.0,
     'L0_attn_b_lambda_q2': 8.0,
     'L0_attn_b_lambda_k1': 8.0,
     'L0_attn_b_lambda_k2': 5.279,
     'L0_ffn_W1': 3.296,
     'L0_ffn_W2': 3.007}
    for name, (base, spread) in spreads.items():
        noise = np.random.default_rng([zlib.crc32(name.encode()), seed]).standard_normal(out[name].shape)
        drawn = base * np.exp(spread * noise) if base else spread * noise
        out[name] = jnp.asarray(drawn.astype(out[name].dtype))
    for name, factor in factors.items():
        out[name] = (out[name] * factor).astype(out[name].dtype)
    return out
```

```python
from contextlib import ExitStack

import numpy as np

import concourse.bass as bass
from concourse import mybir

F32 = mybir.dt.float32
F16 = mybir.dt.float16
BF16 = mybir.dt.bfloat16
I32 = mybir.dt.int32
U32 = mybir.dt.uint32
ALU = mybir.AluOpType
ACT = mybir.ActivationFunctionType
AX = mybir.AxisListType.X

B = 8
S = 512
D = 128
T = B * S
NT = T // 128
NE = 8
FH = 512
FT = NT + NE - 1
SLOTS = FT * 128
ROWW = 258
EPS = 1e-5
BIAS = {"br": (0, 512), "bqkv": (512, 384), "bo": (896, 128), "bg": (1024, 8), "b1": (1032, 4096), "b2": (5128, 1024)}
BIASW = 49
TASKS = 2


class Queues:

    def __init__(self, sem):
        self.sem = sem
        self.count = {}
        self.lists = {"tensor": [], "vector": [], "scalar": [], "gpsimd": [], "sync": []}

    def do(self, engine, make, waits=(), sig=None, inc=1):
        self.lists[engine].append((make, [w for w in waits if w is not None], sig, inc))
        if sig is None:
            return None
        self.count[sig] = self.count.get(sig, 0) + inc
        return (sig, self.count[sig])

    def last(self, sig):
        return (sig, self.count[sig])

    def play(self, engine, eng):
        seen = {}
        for make, waits, sig, inc in self.lists[engine]:
            for name, value in waits:
                if seen.get(name, 0) < value:
                    eng.wait_ge(self.sem(name), value)
                    seen[name] = value
            if make is None:
                continue
            ins = make(eng)
            if sig is not None:
                ins.then_inc(self.sem(sig), inc)


class Ring:

    def __init__(self, banks):
        self.banks = banks
        self.free = [[] for _ in banks]
        self.n = 0

    def take(self):
        i = self.n % len(self.banks)
        self.n += 1
        return i, self.banks[i], list(self.free[i])


def build(nc, a):
    with ExitStack() as ctx:
        def sb(name, shape, dt):
            return ctx.enter_context(nc.sbuf_tensor(name, shape, dt))

        sems = {}

        def sem(name):
            if name not in sems:
                sems[name] = ctx.enter_context(nc.semaphore(name))
            return sems[name]

        q = Queues(sem)
        do = q.do

        ps = ctx.enter_context(nc.psum_tensor("ps", [128, 8, 512], F32))
        ROW = sb("ROW", [128, NT, ROWW], F32)
        TR = sb("TR", [128, 32768], F16)
        STK = sb("STK", [128, 16384], F16)
        V = sb("V", [128, 3, 4, 336], F32)
        P = sb("P", [128, 2, 4, 512], F32)
        BS = sb("BS", [128, BIASW * 128], BF16)
        OR = sb("OR", [128, 2, 512], F32)
        AT = sb("AT", [128, 4, 256], F32)
        ATT = sb("ATT", [128, 2, 512], F32)
        HT = sb("HT", [128, 4, 128], F32)
        WA = sb("WA", [128, 1024], F32)
        WG = sb("WG", [128, NE], F32)
        RT = sb("RT", [128, 3, 512], F32)
        CS = sb("CS", [128, 2, 4, 8], F32)
        idf = sb("idf", [128, 128], F32)
        idh = sb("idh", [128, 128], F16)
        ones = sb("ones", [128, 128], BF16)
        ones3 = sb("ones3", [128, 128], BF16)
        tri = sb("tri", [128, 128], BF16)
        Mb = sb("Mb", [128, 2, 128], F32)
        Mt = sb("Mt", [128, 2, 128], F16)
        st6 = sb("st6", [128, 4, 6], F32)
        mv = sb("mv", [128, 4, 2], F32)
        rs = sb("rs", [128, 4], F32)
        vs = sb("vs", [128, 4], F32)
        half = sb("half", [128, 4], F32)
        rec = sb("rec", [128, 2, 16], F32)
        c8 = sb("c8", [128, NE], F32)
        tio = sb("tio", [128, FT], F32)
        G = sb("G", [128, 6, 32], F32)
        g4 = sb("g4", [128, 4, 4], F32)
        OH = sb("OH", [128, NT, NE], F32)
        OHb = sb("OHb", [128, 4, NE], BF16)
        OFF = sb("OFF", [128, NT + 1, NE], F32)
        rank = sb("rank", [128, NT], F32)
        E8 = sb("E8", [128, 4, NE], F32)
        E8i = sb("E8i", [128, 2, NE], I32)
        slot = sb("slot", [128, NT], U32)
        eoff = sb("eoff", [128, 2, FT], I32)
        ef = sb("ef", [128, 3, FT], F32)
        lam = sb("lam", [128, 4, 8], F32)
        lm = sb("lm", [128, 6], F32)
        bst = sb("bst", [128, 3, BIASW], F32)
        bsp = sb("bsp", [128, 3, BIASW], BF16)
        pad = sb("pad", [128, ROWW], F32)

        xs = [nc.dram_tensor(f"xs{i}", [SLOTS, ROWW], F32, kind="Internal").ap() for i in range(2)]
        x2 = nc.dram_tensor("x2", [T, D], F32, kind="Internal").ap()
        bsd = nc.dram_tensor("bsd", [3, BIASW * 128], BF16, kind="Internal").ap()

        def dma(out, in_, waits=(), sig=None, engine="sync"):
            return do(engine, lambda e: e.dma_start(out, in_), waits, sig, 16)

        x_v = a["x"].rearrange("(t p) d -> p t d", p=128)
        k_b = dma(bst[:, 0, :], a["bias"].rearrange("(p c) -> p c", p=128), sig="ld_bias")
        k_x = []
        for b in range(B):
            k_x.append(dma(ROW[:, 4 * b:4 * b + 4, 128:256], x_v[:, 4 * b:4 * b + 4, :], sig=f"ld_x{b}"))
            if b == 0:
                k_w1 = dma(WA[:, 0:512], a["Wr"], sig="ld_wa")
                for i, n in enumerate(("Wq", "Wk", "Wv", "Wo")):
                    k_w1 = dma(WA[:, 512 + 128 * i:640 + 128 * i], a[n], sig="ld_wa")
        k_g = dma(WG[:, :], a["Wg"], sig="ld_g")
        dma(CS[:, :, :, :], a["cs"], sig="ld_c")
        dma(c8[:, :], a["c8"], sig="ld_c")
        k_c = dma(tio[:, :], a["tio"], sig="ld_c")
        for i, n in enumerate(("lq1", "lk1", "lq2", "lk2")):
            k_l = dma(lam[:, i, :], a[n].rearrange("(a n) -> a n", a=1).broadcast_to([128, 8]), sig="ld_lam")

        do("gpsimd", lambda e: e.memset(idf[:, :], 0.0), sig="cst")
        do("gpsimd", lambda e: e.memset(idh[:, :], 0.0), sig="cst")
        do("gpsimd", lambda e: e.memset(ones[:, :], 1.0), sig="cst")
        do("gpsimd", lambda e: e.memset(half[:, :], -0.5), sig="cst")
        c0 = do("gpsimd", lambda e: e.memset(ones3[:, :], 0.0), sig="cst")
        for m in (idf, idh):
            c1 = do("gpsimd", lambda e, m=m: e.affine_select(out=m[:, :], in_=m[:, :], compare_op=ALU.not_equal, fill=1.0,
                                                             base=0, pattern=[[-1, 128]], channel_multiplier=1), [c0], "cst")
        do("gpsimd", lambda e: e.affine_select(out=tri[:, :], in_=ones[:, :], compare_op=ALU.is_gt, fill=0.0,
                                               base=0, pattern=[[1, 128]], channel_multiplier=-1), [c0], "cst")
        k_cst = do("gpsimd", lambda e: e.memset(ones3[0:3, :], 1.0), [c0], "cst")
        k_bz = do("vector", lambda e: e.memset(BS[:, :].bitcast(U32), 0), sig="bz")
        do("vector", lambda e: e.memset(Mb[:, :, :], 0.0), sig="bz")
        do("vector", lambda e: e.memset(OFF[:, 0, :], 0.0), sig="bz")
        do("vector", lambda e: e.memset(pad[:, 0:257], 0.0), sig="bz")
        k_z = do("vector", lambda e: e.memset(pad[:, 257:258].bitcast(I32), T), sig="bz")
        k_pad = [dma(xs[i].rearrange("(t p) c -> p t c", p=128),
                     pad[:, :].rearrange("p (o c) -> p o c", o=1).broadcast_to([128, FT, ROWW]), [k_z], f"pad{i}",
                     engine="scalar")
                 for i in range(2)]

        w = do("vector", lambda e: e.tensor_copy(bsp[:, 0, :], bst[:, 0, :]), [k_b], "bs")
        w = do("vector", lambda e: e.tensor_tensor(bst[:, 1, :], bst[:, 0, :], bsp[:, 0, :], ALU.subtract), [w], "bs")
        w = do("vector", lambda e: e.tensor_copy(bsp[:, 1, :], bst[:, 1, :]), [w], "bs")
        w = do("vector", lambda e: e.tensor_tensor(bst[:, 2, :], bst[:, 1, :], bsp[:, 1, :], ALU.subtract), [w], "bs")
        w = do("vector", lambda e: e.tensor_copy(bsp[:, 2, :], bst[:, 2, :]), [w], "bs")
        w = dma(bsd.rearrange("r (p c) -> p r c", p=128), bsp[:, :, :], [w], "bsd")
        k_bs = dma(BS[0:3, :], bsd, [w, k_bz], "bsr")

        def bias(name, lo=0, n=None):
            o, length = BIAS[name]
            return BS[:, o + lo:o + lo + (n or length)]

        w = do("vector", lambda e: e.tensor_tensor(lam[:, 0:3:2, :], lam[:, 0:3:2, :], lam[:, 1:4:2, :], ALU.mult), [k_l], "lam")
        w = do("vector", lambda e: e.tensor_reduce(lm[:, 0:2], lam[:, 0:3:2, :], AX, ALU.add), [w], "lam")
        w = do("scalar", lambda e: e.activation(lm[:, 2:4], lm[:, 0:2], ACT.Exp), [w], "lamx")
        w = do("vector", lambda e: e.tensor_tensor(lm[:, 4:5], lm[:, 3:4], lm[:, 2:3], ALU.subtract), [w], "lam")
        k_lam = do("vector", lambda e: e.tensor_scalar(lm[:, 5:6], lm[:, 4:5], -(0.8 - 0.6 * float(np.exp(-0.3 * 0))), None, ALU.add),
                   [w], "lam")

        sring = Ring([0, 1, 2])
        oring = Ring([3])
        mring = Ring([4, 5])
        rring = Ring([6, 7])

        def r16(bank):
            return ps[:, bank, :].bitcast(F16)

        ln_last = [None]

        def layernorm(b, ready):
            t0 = 4 * b
            for i in range(4):
                w = do("vector", lambda e, i=i: e.bn_stats(st6[:, i, :], ROW[:, t0 + i, 128:256]),
                       [ready, ln_last[0]], "lnd")
            for i in range(4):
                w1 = do("vector", lambda e, i=i: e.bn_aggr(mv[:, i, :], st6[:, i, :]), [w], "lnd")
            w = do("gpsimd", lambda e: e.tensor_scalar(vs[:, :], mv[:, :, 1], EPS, None, ALU.add), [w1, k_cst], "lnp")
            w = do("gpsimd", lambda e: e.tensor_tensor(rs[:, :], vs[:, :], half[:, :], ALU.pow), [w], "lnp")
            for i in range(4):
                w2 = do("gpsimd", lambda e, i=i: e.tensor_scalar(ROW[:, t0 + i, 0:128], ROW[:, t0 + i, 128:256],
                                                                mv[:, i, 0:1], rs[:, i:i + 1], ALU.subtract, ALU.mult),
                        [w], "lnp")
            ln_last[0] = w2
            return w2

        def gate(b, ready, ffn):
            t0 = 4 * b
            hw = layernorm(b, ready)
            yield
            _, bank, free = rring.take()
            for i in range(4):
                w = do("tensor", lambda e, i=i: e.transpose(ps[:, bank, 128 * i:128 * i + 128], ROW[:, t0 + i, 0:128], idf[:, :]),
                       free + [hw], "g_t" if i == 3 else None)
            w = do("scalar", lambda e: e.copy(ATT[:, 0, :], ps[:, bank, :]), [w, att_free[0]], "g_c")
            rring.free[rring.n % 2 - 1] = [w]
            yield
            _, bank2, free = rring.take()
            o, n = BIAS["bg"]
            do("tensor", lambda e: e.matmul(ps[:, bank2, 0:32], ones3[:, :],
                                            BS[:, o:o + n].rearrange("p (o n) -> p o n", o=1).broadcast_to([128, 4, NE]),
                                            start=True, stop=False, skip_group_check=True), free + [k_bs])
            for i in range(4):
                w2 = do("tensor", lambda e, i=i: e.matmul(ps[:, bank2, 8 * i:8 * i + 8], ATT[:, 0, 128 * i:128 * i + 128], WG[:, :],
                                                          start=False, stop=(i == 3), skip_group_check=True),
                        [w, k_g], "g_m" if i == 3 else None)
            att_free[0] = w2
            w = do("vector", lambda e: e.tensor_copy(G[:, 0, :], ps[:, bank2, 0:32]), [w2, gate_free[0]], "gd")
            rring.free[rring.n % 2 - 1] = [w]
            lg, dd, ex, vv = (G[:, i, :].rearrange("p (t n) -> p t n", t=4) for i in range(4))

            def bc(x):
                return x.rearrange("p (t o) -> p t o", o=1).broadcast_to([128, 4, NE])

            c8b = c8[:, :].rearrange("p (o n) -> p o n", o=1).broadcast_to([128, 4, NE])
            w = do("vector", lambda e: e.tensor_reduce(g4[:, 0, :], lg, AX, ALU.max), [w], "gd")
            wd = do("vector", lambda e: e.tensor_tensor(dd, lg, bc(g4[:, 0, :]), ALU.subtract), [w], "gd")
            wx = do("scalar", lambda e: e.activation(ex, dd, ACT.Exp), [wd], "gx")
            w = do("vector", lambda e: e.tensor_tensor(vv, lg, bc(g4[:, 0, :]), ALU.is_equal), [w], "gd")
            w = do("vector", lambda e: e.tensor_tensor(vv, vv, c8b, ALU.mult), [w, k_c], "gd")
            w = do("vector", lambda e: e.tensor_reduce(g4[:, 1, :], vv, AX, ALU.max), [w], "gd")
            oh = OH[:, t0:t0 + 4, :]
            w = do("vector", lambda e: e.tensor_tensor(oh, c8b, bc(g4[:, 1, :]), ALU.is_equal), [w, slot_read[0]], "gd")
            wo = do("vector", lambda e: e.tensor_copy(OHb[:, :, :], oh), [w], "gd")
            yield
            w = do("vector", lambda e: e.tensor_reduce(g4[:, 2, :], ex, AX, ALU.add), [wx], "gd")
            w = do("vector", lambda e: e.reciprocal(ROW[:, t0:t0 + 4, 256], g4[:, 2, :]), [w], "gd")
            _, bank3, free = rring.take()
            ohf = OHb[:, :, :].rearrange("p t n -> p (t n)")
            do("tensor", lambda e: e.matmul(ps[:, bank3, 0:32], tri[:, :], ohf, start=True, stop=True), free + [wo])
            w = do("tensor", lambda e: e.matmul(ps[:, bank3, 32:64], ones[:, :], ohf, start=True, stop=True), [], "g_p")
            for i in range(4):
                w = do("vector", lambda e, i=i: e.tensor_tensor(OFF[:, t0 + i + 1, :], OFF[:, t0 + i, :],
                                                               ps[:, bank3, 32 + 8 * i:40 + 8 * i], ALU.add), [w], "gd")
            w = do("vector", lambda e: e.tensor_tensor(dd, ps[:, bank3, 0:32].rearrange("p (t n) -> p t n", t=4), OFF[:, t0:t0 + 4, :],
                                                       ALU.add), [w], "gd")
            rring.free[rring.n % 2 - 1] = [w]
            w = do("vector", lambda e: e.tensor_tensor(dd, dd, oh, ALU.mult), [w], "gd")
            w = do("vector", lambda e: e.tensor_reduce(rank[:, t0:t0 + 4], dd, AX, ALU.add), [w, slot_read[0]], "gd")
            gate_free[0] = w

        att_free = [None]
        gate_free = [None]
        slot_read = [None]

        LA = dict(n=1, gpb=4, kq=120, ks=124, vw=16, one=8, dv=8, scale=float(1.0 / np.sqrt(40.0)))
        LB = dict(n=2, gpb=8, kq=128, ks=128, vw=20, one=16, dv=16, scale=float(8 ** -0.5))

        def attention(L, x_ready, ffn, first):
            one = L["n"] == 1
            gpb, vw, dv = L["gpb"], L["vw"], L["dv"]
            NG = B * gpb
            name = "a" if one else "b"

            def s(x):
                return f"{name}_{x}"

            if one:
                TQ = TR[:, 0:16384].rearrange("p (u t h c) -> p u t h c", u=2, t=4, c=128)
                TK = TR[:, 16384:32768].rearrange("p (u t h c) -> p u t h c", u=2, t=4, c=128)
                SQ = STK[:, 0:8192].rearrange("p (g j n) -> p g j n", g=4, j=4)
                SK = STK[:, 8192:16384].rearrange("p (g j n) -> p g j n", g=4, j=4)
            else:
                TQ = TR[:, 16384:24576].rearrange("p (u t h c) -> p u t h c", u=2, t=4, c=32)
                TK = TR[:, 24576:32768].rearrange("p (u t h c) -> p u t h c", u=2, t=4, c=32)
                SG = STK[:, 0:4096].rearrange("p (g w n) -> p g w n", g=4, w=2)
                SK = STK[:, 4096:12288].rearrange("p (g j n) -> p g j n", g=4, j=4)

            k_v = do("gpsimd", lambda e: e.memset(V[:, :, :, :], 0.0), first, s("init"))
            Vh = V[:, :, :, 0:16 * vw].rearrange("p u t (h c) -> p (u t) h c", c=vw)
            do("gpsimd", lambda e: e.memset(Vh[:, :, :, L["one"]], 1.0), [k_v], s("init"))
            for u in range(2):
                if one:
                    w = do("gpsimd", lambda e, u=u: e.memset(TK[:, u, :, :, 120:124], 0.0), first, s("init"))
                    for j in range(4):
                        k_i = do("gpsimd", lambda e, u=u, j=j: e.memset(TK[:, u, :, j:16:4, 120 + j], 1.0), [w], s("init"))
                else:
                    w = do("gpsimd", lambda e, u=u: e.memset(TQ[:, u, :, :, 24:32], 0.0), first, s("init"))
                    w = do("gpsimd", lambda e, u=u: e.memset(TK[:, u, :, :, 24:32], 0.0), first, s("init"))
                    k_i = do("gpsimd", lambda e, u=u: e.memset(TK[:, u, :, :, 24], 1.0), [w], s("init"))
            k_sz = None
            if not one:
                k_sz = do("vector", lambda e: e.memset(STK[:, 4096:12288].bitcast(U32), 0), first, s("sz"))

            hready = {}
            split_done = {}
            tp_done = {}
            pv_group = {}
            stack = {}
            mrow = {}
            st_group = {}
            smax_tok = {}
            norm_done = {}
            x_done = {}
            m_read = [None, None]
            mt_read = [None, None]
            or_read = [None, None]
            hT_read = [None] * 4
            rt_read = [None]
            at_read = [None]
            rec_read = [None]

            def ln_task(b):
                hready[b] = layernorm(b, x_ready[b])
                return
                yield

            def proj(b, i):
                u, t, hs = b % 2, 4 * b + i, i % 4
                _, bank, free = rring.take()
                w = do("tensor", lambda e: e.transpose(ps[:, bank, 0:128], ROW[:, t, 0:128], idf[:, :]), free + [hready[b], k_cst], s("ht"))
                w = do("scalar", lambda e: e.copy(HT[:, hs, :], ps[:, bank, 0:128]), [w, hT_read[hs]], s("htc"))
                rring.free[rring.n % 2 - 1] = [w]
                hw = w
                tfree = [tp_done.get(b - 2), k_i]
                yield
                if one:
                    _, bk, free = rring.take()
                    do("tensor", lambda e: e.matmul(ps[:, bk, :], ones3[:, :], bias("br"), start=True, stop=False), free + [k_bs])
                    w = do("tensor", lambda e: e.matmul(ps[:, bk, :], HT[:, hs, :], WA[:, 0:512], start=False, stop=True),
                           [hw, k_w1], s("pj"))
                    r = ps[:, bk, :].rearrange("p (h c) -> p h c", c=32)
                    r2 = ps[:, bk, :].rearrange("p (h o c) -> p h o c", o=1, c=32).broadcast_to([128, 16, 2, 32])
                    qq, kk = TQ[:, u, i], TK[:, u, i]
                    wh = do("scalar", lambda e: e.copy(qq[:, :, 0:64].rearrange("p h (o c) -> p h o c", o=2), r2), [w] + tfree, s("hi"))
                    wl = do("vector", lambda e: e.tensor_tensor(qq[:, :, 64:96], r, qq[:, :, 0:32], ALU.subtract), [wh], s("lo"))
                    rring.free[rring.n % 2 - 1] = [wl]
                    do("gpsimd", lambda e: e.tensor_copy(kk[:, :, 0:32], qq[:, :, 0:32]), [wh], s("cp"))
                    do("gpsimd", lambda e: e.tensor_copy(kk[:, :, 64:96], qq[:, :, 32:64]), [wh], s("cp"))
                    wc = do("gpsimd", lambda e: e.tensor_copy(kk[:, :, 32:64], qq[:, :, 64:96]), [wl], s("cp"))
                    yield
                    _, bj, free = rring.take()
                    do("tensor", lambda e: e.matmul(ps[:, bj, 0:384], ones3[:, :], bias("bqkv"), start=True, stop=False), free)
                    w = do("tensor", lambda e: e.matmul(ps[:, bj, 0:384], HT[:, hs, :], WA[:, 512:896], start=False, stop=True),
                           [], s("pj"))
                    hT_read[hs] = w
                    qp = ps[:, bj, 0:128]
                    kp = ps[:, bj, 128:256]
                    vp = ps[:, bj, 256:384].rearrange("p (h c) -> p h c", c=8)

                    def two(x):
                        return x.rearrange("p (h o c) -> p h o c", o=1, c=8).broadcast_to([128, 16, 2, 8])

                    k3 = kk[:, :, 96:128].rearrange("p h (o c) -> p h o c", o=4)[:, :, 0:3:2, :]
                    do("scalar", lambda e: e.copy(qq[:, :, 96:112].rearrange("p h (o c) -> p h o c", o=2), two(qp)), [w], s("hi"))
                    do("scalar", lambda e: e.copy(k3, two(kp)), [], s("hi"))
                    wh = do("scalar", lambda e: e.copy(V[:, b % 3, i, 0:16 * vw].rearrange("p (h c) -> p h c", c=vw)[:, :, 0:8], vp),
                            [pv_group.get(gpb * (b - 2) - 1)], s("hi"))
                    do("vector", lambda e: e.tensor_tensor(qq[:, :, 112:120], qp.rearrange("p (h c) -> p h c", c=8),
                                                           qq[:, :, 96:104], ALU.subtract), [wh], s("lo"))
                    wl = do("vector", lambda e: e.tensor_tensor(kk[:, :, 104:112], kp.rearrange("p (h c) -> p h c", c=8),
                                                                kk[:, :, 96:104], ALU.subtract), [], s("lo"))
                    rring.free[rring.n % 2 - 1] = [wl]
                    split_done[b] = [wl, wh, wc]
                else:
                    _, bk, free = rring.take()
                    w = do("tensor", lambda e: e.matmul(ps[:, bk, :], HT[:, hs, :], WA[:, 0:512], start=True, stop=True),
                           free + [hw, k_w2[0]], s("pj"))
                    pr = ps[:, bk, :].rearrange("p (x c) -> p x c", c=8)

                    def tab(z):
                        return CS[:, z, i, :].rearrange("p (o c) -> p o c", o=1).broadcast_to([128, 64, 8])

                    do("vector", lambda e: e.tensor_tensor(RT[:, 0, :].rearrange("p (x c) -> p x c", c=8), pr, tab(0), ALU.mult),
                       [w, rt_read[0], k_c], s("rot"))
                    wr = do("vector", lambda e: e.tensor_tensor(RT[:, 1, :].rearrange("p (x c) -> p x c", c=8), pr, tab(1), ALU.mult),
                            [], s("rot"))
                    rring.free[rring.n % 2 - 1] = [wr]

                    def part(z, h):
                        return RT[:, z, :].rearrange("p (k h c) -> p k h c", k=2, h=2)[:, :, h, :]

                    do("gpsimd", lambda e: e.tensor_tensor(part(2, 0), part(0, 0), part(1, 1), ALU.subtract), [wr], s("ro2"))
                    wf = do("gpsimd", lambda e: e.tensor_tensor(part(2, 1), part(0, 1), part(1, 0), ALU.add), [], s("ro2"))
                    yield
                    _, bj, free = rring.take()
                    w = do("tensor", lambda e: e.matmul(ps[:, bj, 0:256], HT[:, hs, :], WA[:, 512:768], start=True, stop=True),
                           free, s("pj"))
                    hT_read[hs] = w
                    vo = V[:, b % 3, i, 0:16 * vw].rearrange("p (h c) -> p h c", c=vw)[:, :, 0:16].rearrange("p h (o c) -> p h o c", o=2)
                    vi = ps[:, bj, 0:256].rearrange("p (o h c) -> p h o c", o=2, c=8)
                    wv = do("scalar", lambda e: e.copy(vo, vi), [w, pv_group.get(gpb * (b - 2) - 1), k_i], s("hi"))
                    rring.free[rring.n % 2 - 1] = [wv]
                    fq, fk = RT[:, 2, 0:256], RT[:, 2, 256:512]
                    qq, kk = TQ[:, u, i], TK[:, u, i]

                    def two(x):
                        return x.rearrange("p (h o c) -> p h o c", o=1, c=8).broadcast_to([128, 32, 2, 8])

                    do("scalar", lambda e: e.copy(qq[:, :, 0:16].rearrange("p h (o c) -> p h o c", o=2), two(fq)), [wf] + tfree, s("hi"))
                    wh = do("scalar", lambda e: e.copy(kk.rearrange("p h (o c) -> p h o c", o=4)[:, :, 0:3:2, :], two(fk)), [], s("hi"))
                    do("gpsimd", lambda e: e.tensor_tensor(qq[:, :, 16:24], fq.rearrange("p (h c) -> p h c", c=8), qq[:, :, 0:8],
                                                           ALU.subtract), [wh], s("lo"))
                    wl = do("gpsimd", lambda e: e.tensor_tensor(kk[:, :, 8:16], fk.rearrange("p (h c) -> p h c", c=8), kk[:, :, 0:8],
                                                                ALU.subtract), [], s("lo"))
                    rt_read[0] = wl
                    split_done[b] = [wl, wh, wv]

            def group(g):
                b, gl, sl = g // gpb, g % gpb, g % 4
                u = b % 2
                gfree = [st_group.get(g - 4)]
                if one:
                    for j2 in range(2):
                        for T_, K_, S_ in ((TQ, 120, SQ), (TK, 124, SK)):
                            _, bank, free = rring.take()
                            for jj in range(2):
                                for i in range(4):
                                    h = 4 * gl + 2 * j2 + jj
                                    w = do("tensor", lambda e, h=h, i=i, jj=jj, T_=T_, K_=K_, bank=bank: e.transpose(
                                        r16(bank)[0:K_, 512 * jj + 128 * i:512 * jj + 128 * i + 128], T_[:, u, i, h, 0:K_], idh[:, :]),
                                        free + split_done[b], s("tp") if jj + i == 4 else None)
                            w2 = do("scalar", lambda e, j2=j2, K_=K_, S_=S_, bank=bank: e.copy(
                                S_[0:K_, sl, 2 * j2:2 * j2 + 2, :], r16(bank)[0:K_, :].rearrange("p (j n) -> p j n", j=2)),
                                [w] + gfree, s("tpc"))
                            rring.free[rring.n % 2 - 1] = [w2]
                            yield
                    stack[g] = [w2]
                else:
                    _, bank, free = rring.take()
                    for z, T_ in ((0, TQ), (1, TK)):
                        for i in range(4):
                            w = do("tensor", lambda e, z=z, i=i, T_=T_: e.transpose(
                                r16(bank)[:, 512 * z + 128 * i:512 * z + 128 * i + 128],
                                T_[:, u, i, 4 * gl:4 * gl + 4, :].rearrange("p h c -> p (h c)"), idh[:, :]),
                                free + split_done[b], s("tp") if z + i == 4 else None)
                    w2 = do("scalar", lambda e: e.copy(SG[:, sl], r16(bank).rearrange("p (w n) -> p w n", w=2)), [w] + gfree, s("tpc"))
                    rring.free[rring.n % 2 - 1] = [w2]
                    for j in range(4):
                        w3 = dma(SK[32 * j:32 * j + 32, sl, j, :], SG[32 * j:32 * j + 32, sl, 1, :], [w2, k_sz], s(f"msk{sl}"))
                    stack[g] = [w2, w3]
                if gl == gpb - 1:
                    tp_done[b] = w

            def smax(g, j, qt):
                sl = g % 4
                ri, bank, free = mring.take()
                if one:
                    l_, r_ = SQ[0:120, sl, j, 128 * qt:128 * qt + 128], SK[0:120, sl, j, :]
                else:
                    l_, r_ = SG[:, sl, 0, 128 * qt:128 * qt + 128], SK[:, sl, j, :]
                w = do("tensor", lambda e: e.matmul(ps[:, bank, :], l_, r_, start=True, stop=True), free + stack[g], s("sm"))
                c = 32 * qt + j
                w2 = do("vector", lambda e: e.tensor_reduce(Mb[:, g % 2, c:c + 1], ps[:, bank, :], AX, ALU.max),
                        [w, m_read[g % 2]], s("mx"))
                mring.free[ri] = [w2]
                smax_tok[g] = (w, w2)

            def mrows(g):
                sl, z = g % 4, g % 2
                ri, bank, free = rring.take()
                w = do("tensor", lambda e: e.transpose(ps[:, bank, 0:128], Mb[:, z, :], idf[:, :]), free + [smax_tok[g][1]], s("mt"))
                m_read[z] = w
                w2 = do("scalar", lambda e: e.mul(Mt[:, z, :], ps[:, bank, 0:128], -1.0), [w, mt_read[z]], s("mc"))
                rring.free[ri] = [w2]
                for qt in range(4):
                    src = Mt[32 * qt:32 * qt + 4, z, :]
                    if one:
                        dst = SQ[120:124, sl, :, 128 * qt:128 * qt + 128]
                        src = src.rearrange("p (o n) -> p o n", o=1).broadcast_to([4, 4, 128])
                    else:
                        dst = SG[24:128:32, sl, 0, 128 * qt:128 * qt + 128]
                    w3 = dma(dst, src, [w2, smax_tok[g][0]], s(f"mr{z}"))
                mt_read[z] = w3
                mrow[g] = w3
                return
                yield

            def scores(g, kt, j):
                sl = g % 4
                si, bank, free = sring.take()
                if one:
                    l_, r_ = SK[0:124, sl, j, 128 * kt:128 * kt + 128], SQ[0:124, sl, j, :]
                else:
                    l_, r_ = SK[:, sl, j, 128 * kt:128 * kt + 128], SG[:, sl, 0, :]
                w = do("tensor", lambda e: e.matmul(ps[:, bank, :], l_, r_, start=True, stop=True), free + [mrow[g]], s("st"))
                st_group[g] = w
                z = (4 * g + kt) % 2
                w2 = do("scalar", lambda e: e.activation(P[:, z, j, :], ps[:, bank, :], ACT.Exp, scale=L["scale"]),
                        [w, pv_tok.get(4 * g + kt - 2)], s("exp"))
                sring.free[si] = [w2]
                exp_tok[4 * g + kt] = w2

            exp_tok = {}
            pv_tok = {}
            o_use = {}

            def pv(st):
                g, kt = st // 4, st % 4
                b, hh = g // gpb, (g % gpb) % 4
                if kt == 0:
                    o_use[g] = oring.take()
                oi, bank, free = o_use[g]
                for j in range(4):
                    h = 4 * hh + j
                    w = do("tensor", lambda e, j=j, h=h: e.matmul(ps[32 * j:32 * j + 32, bank, :], V[:, b % 3, kt, vw * h:vw * h + 32],
                                                                  P[:, st % 2, j, :], start=(kt == 0), stop=(kt == 3)),
                           (free if kt == 0 else []) + [exp_tok[st]] + split_done[b], s("pv") if j == 3 else None)
                pv_tok[st] = w
                if kt == 3:
                    pv_group[g] = w

            def norm(g):
                oi, bank, _ = o_use[g]
                z, gl = g % 2, g % gpb
                hh = gl % 4
                w = do("scalar", lambda e: e.copy(OR[:, z, :], ps[:, bank, :]), [pv_group[g], or_read[z]], s("oc"))
                oring.free[oi] = [w]
                yield
                ri, rb, free = rring.take()
                for i in range(4):
                    w1 = do("tensor", lambda e, i=i: e.transpose(ps[:, rb, 128 * i:128 * i + 128], OR[:, z, 128 * i:128 * i + 128], idf[:, :]),
                            free + [w], s("ot") if i == 3 else None)
                or_read[z] = w1
                o4 = ps[:, rb, :].rearrange("p (t j c) -> p t j c", t=4, j=4)
                rc = rec[:, 0, :].rearrange("p (t j) -> p t j", t=4)
                w2 = do("vector", lambda e: e.reciprocal(rc, o4[:, :, :, L["one"]]), [w1, rec_read[0]], s("nm"))
                c0 = hh * 4 * dv
                ao = AT[:, :, c0:c0 + 4 * dv].rearrange("p t (j c) -> p t j c", j=4)
                if gl < 4:
                    rb4 = rec[:, 0, :].rearrange("p (t j o) -> p t j o", t=4, o=1).broadcast_to([128, 4, 4, dv])
                    w3 = do("vector", lambda e: e.tensor_tensor(ao, o4[:, :, :, 0:dv], rb4, ALU.mult), [w2, at_read[0]], s("nm"))
                    rring.free[ri] = [w3]
                else:
                    w3 = do("vector", lambda e: e.tensor_scalar(rec[:, 1, :], rec[:, 0, :], lm[:, 5:6], None, ALU.mult), [w2, k_lam], s("nm"))
                    rb4 = rec[:, 1, :].rearrange("p (t j o) -> p t j o", t=4, o=1).broadcast_to([128, 4, 4, dv])
                    tmp = RT[:, 0, 0:256].rearrange("p (t j c) -> p t j c", t=4, j=4)
                    tmp = OT[:, :].rearrange("p (t j c) -> p t j c", t=4, j=4)
                    w3 = do("vector", lambda e: e.tensor_tensor(tmp, o4[:, :, :, 0:dv], rb4, ALU.mult), [w3], s("nm"))
                    rring.free[ri] = [w3]
                    w3 = do("vector", lambda e: e.tensor_tensor(ao, ao, tmp, ALU.add), [w3], s("nm"))
                rec_read[0] = w3
                norm_done[g] = w3

            def out(b):
                nd = norm_done[gpb * (b + 1) - 1]
                nch = 1 if one else 2
                for c in range(nch):
                    ri, bank, free = rring.take()
                    for i in range(4):
                        w = do("tensor", lambda e, i=i, c=c, bank=bank: e.transpose(ps[:, bank, 128 * i:128 * i + 128],
                                                                                    AT[:, i, 128 * c:128 * c + 128], idf[:, :]),
                               free + [nd], s("at") if i == 3 else None)
                    w2 = do("scalar", lambda e, c=c, bank=bank: e.copy(ATT[:, c, :], ps[:, bank, :]), [w, att_free[0]], s("atc"))
                    rring.free[ri] = [w2]
                at_read[0] = w
                yield
                ri, bank, free = rring.take()
                if one:
                    o, n = BIAS["bo"]
                    do("tensor", lambda e: e.matmul(ps[:, bank, :], ones3[:, :],
                                                    BS[:, o:o + n].rearrange("p (o n) -> p o n", o=1).broadcast_to([128, 4, 128]),
                                                    start=True, stop=False, skip_group_check=True), free)
                    for i in range(4):
                        w = do("tensor", lambda e, i=i: e.matmul(ps[:, bank, 128 * i:128 * i + 128], ATT[:, 0, 128 * i:128 * i + 128],
                                                                 WA[:, 896:1024], start=False, stop=(i == 3), skip_group_check=True),
                               [w2], s("op") if i == 3 else None)
                else:
                    for i in range(4):
                        for c in range(2):
                            w = do("tensor", lambda e, i=i, c=c: e.matmul(ps[:, bank, 128 * i:128 * i + 128],
                                                                          ATT[:, c, 128 * i:128 * i + 128],
                                                                          WA[:, 768 + 128 * c:896 + 128 * c], start=(c == 0), stop=(c == 1)),
                                   free + [w2], s("op") if i == 3 and c == 1 else None)
                att_free[0] = w
                xr = ROW[:, 4 * b:4 * b + 4, 128:256]
                w = do("vector", lambda e: e.tensor_tensor(xr, xr, ps[:, bank, :].rearrange("p (t n) -> p t n", t=4), ALU.add),
                       [w], s("res"))
                rring.free[ri] = [w]
                x_done[b] = w
                yield
                yield from gate(b, w, ffn)

            tasks = []

            def start(due, task):
                tasks.append((due, len(tasks), task))
                tasks.sort(key=lambda x: x[0])

            def advance(most):
                for t in list(tasks)[:most]:
                    try:
                        next(t[2])
                    except StopIteration:
                        tasks.remove(t)

            per = gpb // 4
            for win in range(-3 - gpb, NG + 1):
                pb, pi = divmod(win + 3 + gpb, gpb)
                if pb < B:
                    if pi == 0:
                        start(win, ln_task(pb))
                        advance(1)
                    if pi % per == 0:
                        start(win + per, proj(pb, pi // per))
                if 0 <= win + 1 < NG:
                    start(win, mrows(win + 1))
                if 0 <= win + 3 < NG:
                    start(win + 0.5, group(win + 3))
                for kt in range(4):
                    live, ahead = 0 <= win < NG, 0 <= win + 2 < NG
                    for j in range(4):
                        if live:
                            scores(win, kt, j)
                        if ahead:
                            smax(win + 2, j, kt)
                        if j % 2:
                            advance(TASKS)
                    st = 4 * win + kt - 1
                    if 0 <= st < 4 * NG:
                        pv(st)
                        if st % 4 == 3:
                            t = norm(st // 4)
                            next(t)
                            start(win + 0.7, t)
                    if kt == 2 and win >= 1 and win % gpb == 0:
                        start(win + gpb, out(win // gpb - 1))
                while any(t[0] < win + 1 for t in tasks) or (tasks and (win < -2 or win == NG)):
                    advance(8)
            return x_done

        OT = sb("OT", [128, 256], F32)
        k_w2 = [None]

        def experts(n, dst):
            Cn = OFF[:, NT, :]
            w = gate_free[0]
            w = do("vector", lambda e: e.tensor_scalar(E8i[:, 0, :], Cn, 127.0, None, ALU.add), [w], "rt")
            w = do("vector", lambda e: e.tensor_scalar(E8i[:, 1, :], E8i[:, 0, :], 7, None, ALU.logical_shift_right), [w], "rt")
            w = do("vector", lambda e: e.tensor_copy(E8[:, 0, :], E8i[:, 1, :]), [w], "rt")
            w = do("vector", lambda e: e.tensor_copy(E8[:, 1, :], E8[:, 0, :]), [w], "rt")
            for k in range(1, NE):
                w = do("vector", lambda e, k=k: e.tensor_tensor(E8[:, 1, k:k + 1], E8[:, 1, k - 1:k], E8[:, 0, k:k + 1], ALU.add), [w], "rt")
            wc = w
            w = do("vector", lambda e: e.tensor_tensor(E8[:, 2, :], E8[:, 1, :], E8[:, 0, :], ALU.subtract), [w], "rt")
            w = do("vector", lambda e: e.tensor_scalar(E8[:, 3, :], E8[:, 2, :], 128.0, None, ALU.mult), [w], "rt")
            big = RT[:, 0, 0:256].rearrange("p (t n) -> p t n", t=NT)
            w = do("vector", lambda e: e.tensor_tensor(big, OH[:, :, :], E8[:, 3, :].rearrange("p (o n) -> p o n", o=1).broadcast_to([128, NT, NE]),
                                                       ALU.mult), [w], "rt")
            w = do("vector", lambda e: e.tensor_reduce(RT[:, 1, 0:NT], big, AX, ALU.add), [w], "rt")
            ws = do("vector", lambda e: e.tensor_tensor(slot[:, :], rank[:, :], RT[:, 1, 0:NT], ALU.add), [w], "rt")
            slot_read[0] = ws
            w_idx = do("gpsimd", lambda e: e.iota(ROW[:, :, 257].bitcast(I32), pattern=[[128, NT]], base=0, channel_multiplier=1), [], "idx")
            for t in range(NT):
                w_sc = do("gpsimd", lambda e, t=t: e.indirect_dma_start(
                    out=xs[n][:, :], out_offset=bass.IndirectOffsetOnAxis(ap=slot[:, t:t + 1], axis=0),
                    in_=ROW[:, t, 0:ROWW], in_offset=None), [ws, w_idx, k_pad[n]], f"scat{n}", 16)
            cmp = RT[:, 2, 0:FT * NE].rearrange("p (t n) -> p t n", n=NE)
            tb = tio[:, :].rearrange("p (t o) -> p t o", o=1).broadcast_to([128, FT, NE])
            cb = E8[:, 1, :].rearrange("p (o n) -> p o n", o=1).broadcast_to([128, FT, NE])
            w = do("vector", lambda e: e.tensor_tensor(cmp, cb, tb, ALU.is_le), [wc, k_c], "rt")
            w = do("vector", lambda e: e.tensor_reduce(ef[:, 0, :], cmp, AX, ALU.add), [w], "rt")
            w = do("vector", lambda e: e.tensor_scalar(ef[:, 1, :], ef[:, 0, :], float(NE - 1), None, ALU.min), [w], "rt")
            do("vector", lambda e: e.tensor_scalar(eoff[:, 0, :], ef[:, 1, :], float(FH), None, ALU.mult), [w], "rt")
            we = do("vector", lambda e: e.tensor_scalar(eoff[:, 1, :], ef[:, 1, :], float(D), None, ALU.mult), [w], "rt")

            W1 = TR[:, 0:8192].bitcast(F32)
            W2 = TR[:, 8192:16384].bitcast(F32)
            if n == 0:
                k_e[0] = [dma(W1[:, :], a["W1"], ffn_first, "ld_w1", engine="scalar"),
                          dma(W2[:, :], a["W2"], [], "ld_w2", engine="scalar")]
                k_w2[0] = dma(WA[:, 0:768], a["Wqkv"], ffn_first, "ld_wb", engine="scalar")
                k_w2[0] = dma(WA[:, 768:1024].rearrange("p (c n) -> p c n", c=2), a["Wproj"], [], "ld_wb", engine="scalar")

            fP = P[:, :, :, :].rearrange("p z j n -> p (z j n)")
            X = [STK[:, 520 * i:520 * i + 516].bitcast(F32) for i in range(6)]
            XT = [STK[:, 4096 + 256 * i:4352 + 256 * i].bitcast(F32) for i in range(3)]
            Y = [STK[:, 5120 + 256 * i:5376 + 256 * i].bitcast(F32) for i in range(6)]
            A = [fP[:, 512 * i:512 * i + 512] for i in range(3)]
            A2 = [fP[:, 2048 + 512 * i:2560 + 512 * i] for i in range(3)]
            ring = Ring([0, 1, 2, 3, 4, 5, 6, 7])
            ld, xt, ups, act, at2, yy, sc = {}, {}, {}, {}, {}, {}, {}
            xt_r, a_r, a2_r = {}, {}, {}
            out_tok = []

            def load(t):
                ld[t] = dma(X[t % 6], xs[n][128 * t:128 * t + 128, :], [w_sc, sc.get(t - 6), yy.get(t - 6)] + ffn_first, f"ldx{t % 6}")

            def s0(t):
                ri, bank, free = ring.take()
                w = do("tensor", lambda e: e.transpose(ps[:, bank, 0:128], X[t % 6][:, 0:128], idf[:, :]), free + [ld[t]], "f_t")
                xt[t] = do("vector", lambda e: e.tensor_copy(XT[t % 3], ps[:, bank, 0:128]), [w, xt_r.get(t - 3)], "f_d")
                ring.free[ri] = [xt[t]]

            def s1(t):
                ri, bank, free = ring.take()

                def up(e):
                    v = e.value_load(eoff[0:1, 0, t:t + 1], min_val=0, max_val=(NE - 1) * FH)
                    o = BIAS["b1"][0]
                    e.matmul(ps[:, bank, :], ones3[:, :], BS[:, bass.ds(v + o, FH)], start=True, stop=False)
                    return e.matmul(ps[:, bank, :], XT[t % 3], W1[:, bass.ds(v, FH)], start=False, stop=True)

                w = do("tensor", up, free + [xt[t], we] + k_e[0], "f_u")
                xt_r[t] = w
                act[t] = do("scalar", lambda e: e.activation(A[t % 3], ps[:, bank, :], ACT.Silu), [w, a_r.get(t - 3)] + ffn_first, "f_s")
                ring.free[ri] = [act[t]]

            def s2(t):
                ri, bank, free = ring.take()
                for c in range(4):
                    w = do("tensor", lambda e, c=c: e.transpose(ps[:, bank, 128 * c:128 * c + 128], A[t % 3][:, 128 * c:128 * c + 128], idf[:, :]),
                           free + [act[t]], "f_at" if c == 3 else None)
                a_r[t] = w
                at2[t] = do("vector", lambda e: e.tensor_copy(A2[t % 3], ps[:, bank, :]), [w, a2_r.get(t - 3)] + ffn_first, "f_d")
                ring.free[ri] = [at2[t]]

            def s3(t):
                ri, bank, free = ring.take()

                def down(e):
                    v = e.value_load(eoff[0:1, 0, t:t + 1], min_val=0, max_val=(NE - 1) * FH)
                    v2 = e.value_load(eoff[0:1, 1, t:t + 1], min_val=0, max_val=(NE - 1) * D)
                    o = BIAS["b2"][0]
                    e.matmul(ps[:, bank, 0:128], ones3[:, :], BS[:, bass.ds(v2 + o, D)], start=True, stop=False)
                    for c in range(4):
                        m = e.matmul(ps[:, bank, 0:128], A2[t % 3][:, 128 * c:128 * c + 128], W2[:, bass.ds(v + 128 * c, D)],
                                     start=False, stop=(c == 3))
                    return m

                w = do("tensor", down, free + [at2[t]], "f_o")
                a2_r[t] = w
                yy[t] = do("vector", lambda e: e.scalar_tensor_tensor(out=Y[t % 6], in0=ps[:, bank, 0:128], scalar=X[t % 6][:, 256:257],
                                                                      in1=X[t % 6][:, 128:256], op0=ALU.mult, op1=ALU.add),
                           [w, sc.get(t - 6)], "f_d")
                ring.free[ri] = [yy[t]]
                sc[t] = do("gpsimd", lambda e: e.indirect_dma_start(
                    out=dst[:, :], out_offset=bass.IndirectOffsetOnAxis(ap=X[t % 6][:, 257:258].bitcast(U32), axis=0),
                    in_=Y[t % 6], in_offset=None, bounds_check=T - 1, oob_is_err=False), [yy[t]], f"so{n}_{t % 6}", 16)

            for t in range(4):
                load(t)
            for step in range(FT + 3):
                if 0 <= step - 3 < FT:
                    s3(step - 3)
                if step + 4 < FT and step >= 0:
                    pass
                if 0 <= step - 2 < FT:
                    s2(step - 2)
                if 0 <= step - 1 < FT:
                    s1(step - 1)
                if step < FT:
                    s0(step)
                if 4 <= step + 3 and step + 3 < FT and step + 3 >= 4:
                    load(step + 3)
            for r in (sring, oring, mring, rring):
                r.free = [ring.free[i] for i in r.banks]
            return [sc[t] for t in range(FT - 6, FT)], [q.last("f_o"), q.last("f_d"), q.last("f_s")]

        k_e = [None]
        ffn_first = []
        x1 = attention(LA, k_x, 0, [])
        ffn_first = [q.last("a_st"), q.last("a_pv"), q.last("a_tp"), q.last("a_op"), q.last("a_exp"), q.last("a_pj"), q.last("a_sm")]
        end0, rest0 = experts(0, x2)
        x2_v = x2.rearrange("(t p) d -> p t d", p=128)
        k_x2 = []
        for b in range(B):
            k_x2.append(dma(ROW[:, 4 * b:4 * b + 4, 128:256], x2_v[:, 4 * b:4 * b + 4, :], end0 + [q.last("scat0")], f"ld_xx{b}"))
        x3 = attention(LB, k_x2, 1, ffn_first + rest0 + end0)
        ffn_first = [q.last("b_st"), q.last("b_pv"), q.last("b_tp"), q.last("b_op"), q.last("b_exp"), q.last("b_pj"), q.last("b_sm")]
        end1, _ = experts(1, a["out"])
        do("gpsimd", None, end1)

        block = ctx.enter_context(nc.Block())

        @block.sync
        def _(eng):
            q.play("sync", eng)

        @block.gpsimd
        def _(eng):
            q.play("gpsimd", eng)

        @block.scalar
        def _(eng):
            q.play("scalar", eng)

        @block.vector
        def _(eng):
            q.play("vector", eng)

        @block.tensor
        def _(eng):
            q.play("tensor", eng)


def tables():
    inv = (np.float32(1.0) / np.power(np.float32(10000.0), np.arange(0, 16, 2, dtype=np.float32) / np.float32(16))).astype(np.float32)
    f = (np.arange(S, dtype=np.float32)[:, None] * inv[None, :]).astype(np.float32)
    cs = np.stack([np.cos(f), np.sin(f)]).astype(np.float32)
    cs = np.ascontiguousarray(cs.reshape(2, 4, 128, 8).transpose(2, 0, 1, 3))
    c8 = np.tile(np.arange(NE, 0, -1, dtype=np.float32), (128, 1))
    tio = np.tile(np.arange(FT, dtype=np.float32), (128, 1))
    return cs, c8, tio


def kernel(**inputs):
    import concourse.bacc as bacc
    from concourse.bass_utils import run_bass_kernel_spmd

    i = {k: np.asarray(v) for k, v in inputs.items()}
    pa, pb, pf = "L0_attn_a_", "L0_attn_b_", "L0_ffn_"
    cs, c8, tio = tables()
    bias = np.concatenate([i[pa + "br"], i[pa + "bq"], i[pa + "bk"], i[pa + "bv"], i[pa + "bo"], i[pf + "bg"],
                           i[pf + "b1"].reshape(-1), i[pf + "b2"].reshape(-1)])
    bias = np.concatenate([bias, np.zeros(BIASW * 128 - bias.shape[0], bias.dtype)])
    arrays = {
        "x": i[pa + "x"].reshape(T, D), "Wq": i[pa + "Wq"], "Wk": i[pa + "Wk"], "Wv": i[pa + "Wv"], "Wr": i[pa + "Wr"],
        "Wo": i[pa + "Wo"], "bias": bias, "Wg": i[pf + "Wg"],
        "W1": i[pf + "W1"].transpose(1, 0, 2).reshape(D, NE * FH),
        "W2": i[pf + "W2"].reshape(NE, 4, 128, D).transpose(2, 0, 1, 3).reshape(128, NE * 4 * D),
        "Wqkv": i[pb + "W_qkv"].T, "Wproj": i[pb + "W_proj"].T.reshape(2, 128, D).transpose(1, 0, 2),
        "lq1": i[pb + "lambda_q1"], "lk1": i[pb + "lambda_k1"], "lq2": i[pb + "lambda_q2"], "lk2": i[pb + "lambda_k2"],
        "cs": cs, "c8": c8, "tio": tio,
    }
    arrays = {f"in_{k}": np.ascontiguousarray(v) for k, v in arrays.items()}
    nc = bacc.Bacc("TRN2", target_bir_lowering=False, num_devices=1)
    aps = {k[3:]: nc.dram_tensor(k, v.shape, mybir.dt.from_np(v.dtype), kind="ExternalInput").ap() for k, v in arrays.items()}
    aps["out"] = nc.dram_tensor("out0", (T, D), F32, kind="ExternalOutput").ap()
    build(nc, aps)
    r = run_bass_kernel_spmd(nc, [arrays], core_ids=[0])
    return r.results[0]["out0"].reshape(B, S, D)
```

```python
from contextlib import ExitStack

import numpy as np

import concourse.bass as bass
from concourse import mybir

F32 = mybir.dt.float32
F16 = mybir.dt.float16
BF16 = mybir.dt.bfloat16
I32 = mybir.dt.int32
U32 = mybir.dt.uint32
ALU = mybir.AluOpType
ACT = mybir.ActivationFunctionType
AX = mybir.AxisListType.X

B = 8
S = 512
D = 128
T = B * S
NT = T // 128
NE = 8
FH = 512
FT = NT + NE - 1
REG = T + 128
SLOTS = NE * REG + (NE - 1) * 128
ROWW = 258
EPS = 1e-5
BIAS = {"br": (0, 512), "bqkv": (512, 384), "bo": (896, 128), "bg": (1024, 8), "b1": (1032, 4096), "b2": (5128, 1024)}
BIASW = 49


class Queues:

    PRICE = {"tensor": (4, 0.42), "vector": (65, 1.05), "scalar": (55, 0.83), "gpsimd": (100, 2.5), "sync": (0, 1.0)}
    SIGNAL = 170
    DMA = 1900

    def __init__(self, sem):
        self.sem = sem
        self.count = {}
        self.lists = {"tensor": [], "vector": [], "scalar": [], "gpsimd": [], "sync": []}
        self.clock = {e: 0.0 for e in self.lists}
        self.due = {}

    def do(self, engine, make, waits=(), sig=None, inc=1, n=128):
        waits = [w for w in waits if w is not None]
        self.lists[engine].append((make, waits, sig, inc))
        fixed, each = self.PRICE[engine]
        self.clock[engine] = max(self.clock[engine], self.when(waits)) + fixed + each * n
        if sig is None:
            return None
        self.count[sig] = self.count.get(sig, 0) + inc
        self.due[sig, self.count[sig]] = self.clock[engine] + (self.DMA if inc == 16 else self.SIGNAL)
        return (sig, self.count[sig])

    def when(self, tokens):
        return max((self.due[t] for t in tokens if t is not None), default=0.0)

    def last(self, sig):
        return (sig, self.count[sig])

    def run(self, streams):
        heads = [[s, h] for s, h in ((s, next(s, None)) for s in streams) if h is not None]
        while heads:
            best = None
            for i, (s, h) in enumerate(heads):
                if h[1] is None:
                    h = heads[i][1] = next(s, None)
                    if h is None:
                        best = None
                        break
                if h[1] is not None:
                    key = (max(self.clock["tensor"], self.when(h[1])), h[0])
                    if best is None or key < best[0]:
                        best = (key, i)
            else:
                if best is None:
                    raise RuntimeError("no stage can be queued")
                i = best[1]
                heads[i][1] = next(heads[i][0], None)
            if heads[i][1] is None:
                heads.pop(i)

    def play(self, engine, eng):
        seen = {}
        for make, waits, sig, inc in self.lists[engine]:
            for name, value in waits:
                if seen.get(name, 0) < value:
                    eng.wait_ge(self.sem(name), value)
                    seen[name] = value
            if make is None:
                continue
            ins = make(eng)
            if sig is not None:
                ins.then_inc(self.sem(sig), inc)


class Ring:

    def __init__(self, banks):
        self.banks = banks
        self.free = [[] for _ in banks]
        self.idle = list(range(len(banks)))

    def take(self, rank, waits=()):
        waits = list(waits)
        while True:
            if not self.idle:
                yield rank, None
                continue
            i = self.idle[0]
            yield rank, self.free[i] + waits
            if self.idle and self.idle[0] == i:
                self.idle.pop(0)
                return i, self.banks[i], list(self.free[i])

    def give(self, i, tokens):
        self.free[i] = tokens
        self.idle.append(i)


def build(nc, a):
    with ExitStack() as ctx:
        def sb(name, shape, dt):
            return ctx.enter_context(nc.sbuf_tensor(name, shape, dt))

        sems = {}

        def sem(name):
            if name not in sems:
                sems[name] = ctx.enter_context(nc.semaphore(name))
            return sems[name]

        q = Queues(sem)
        do = q.do

        ps = ctx.enter_context(nc.psum_tensor("ps", [128, 8, 512], F32))
        ROW = sb("ROW", [128, NT, ROWW], F32)
        TR = sb("TR", [128, 32768], F16)
        STK = sb("STK", [128, 16384], F16)
        V = sb("V", [128, 3, 4, 336], F32)
        P = sb("P", [128, 2, 4, 512], F32)
        BS = sb("BS", [128, BIASW * 128], BF16)
        OR = sb("OR", [128, 2, 512], F32)
        AT = sb("AT", [128, 4, 256], F32)
        ATT = sb("ATT", [128, 2, 512], F32)
        HT = sb("HT", [128, 4, 128], F32)
        WA = sb("WA", [128, 1024], F32)
        WG = sb("WG", [128, NE], F32)
        RT = sb("RT", [128, 3, 512], F32)
        CS = sb("CS", [128, 2, 4, 8], F32)
        idf = sb("idf", [128, 128], F32)
        idh = sb("idh", [128, 128], F16)
        ones = sb("ones", [128, 128], BF16)
        ones3 = sb("ones3", [128, 128], BF16)
        tri = sb("tri", [128, 128], BF16)
        Mb = sb("Mb", [128, 2, 128], F32)
        Mt = sb("Mt", [128, 2, 128], F16)
        st6 = sb("st6", [128, 2, 4, 6], F32)
        mv = sb("mv", [128, 2, 4, 2], F32)
        rs = sb("rs", [128, 2, 4], F32)
        vs = sb("vs", [128, 2, 4], F32)
        half = sb("half", [128, 4], F32)
        rec = sb("rec", [128, 2, 16], F32)
        c8 = sb("c8", [128, NE], F32)
        e4 = sb("e4", [128, NE], F32)
        tio = sb("tio", [128, FT], F32)
        G = sb("G", [128, 6, 32], F32)
        g4 = sb("g4", [128, 4, 4], F32)
        OH = sb("OH", [128, NT, NE], F32)
        OHb = sb("OHb", [128, 4, NE], BF16)
        OFF = sb("OFF", [128, NT + 1, NE], F32)
        E8 = sb("E8", [128, 4, NE], F32)
        E8i = sb("E8i", [128, 2, NE], I32)
        slot = sb("slot", [128, NT], U32)
        eoff = sb("eoff", [128, 2, FT], I32)
        ri = sb("ri", [128, FT + NE], I32)
        ef = sb("ef", [128, 3, FT], F32)
        lam = sb("lam", [128, 4, 8], F32)
        lm = sb("lm", [128, 6], F32)
        bst = sb("bst", [128, 3, BIASW], F32)
        bsp = sb("bsp", [128, 3, BIASW], BF16)
        pad = sb("pad", [128, ROWW], F32)

        xs = [nc.dram_tensor(f"xs{i}", [SLOTS, ROWW], F32, kind="Internal").ap() for i in range(2)]
        x2 = nc.dram_tensor("x2", [T, D], F32, kind="Internal").ap()
        bsd = nc.dram_tensor("bsd", [3, BIASW * 128], BF16, kind="Internal").ap()

        def dma(out, in_, waits=(), sig=None, engine="sync", n=650):
            return do(engine, lambda e: e.dma_start(out, in_), waits, sig, 16, n)

        x_v = a["x"].rearrange("(t p) d -> p t d", p=128)
        k_x = [dma(ROW[:, 0:4, 128:256], x_v[:, 0:4, :], sig="ld_x0")]
        k_b = dma(bst[:, 0, :], a["bias"].rearrange("(p c) -> p c", p=128), sig="ld_bias")
        k_w1 = dma(WA[:, 0:512], a["Wr"], sig="ld_wa")
        for i, n in enumerate(("Wq", "Wk", "Wv", "Wo")):
            k_w1 = dma(WA[:, 512 + 128 * i:640 + 128 * i], a[n], sig="ld_wa")
        do("gpsimd", lambda e: e.memset(idf[:, :], 0.0), sig="cst")
        do("gpsimd", lambda e: e.memset(idh[:, :], 0.0), sig="cst")
        do("gpsimd", lambda e: e.memset(ones[:, :], 1.0), sig="cst")
        do("gpsimd", lambda e: e.memset(half[:, :], -0.5), sig="cst")
        c0 = do("gpsimd", lambda e: e.memset(ones3[:, :], 0.0), sig="cst")
        for m in (idf, idh):
            c1 = do("gpsimd", lambda e, m=m: e.affine_select(out=m[:, :], in_=m[:, :], compare_op=ALU.not_equal, fill=1.0,
                                                             base=0, pattern=[[-1, 128]], channel_multiplier=1), [c0], "cst")
        do("gpsimd", lambda e: e.affine_select(out=tri[:, :], in_=ones[:, :], compare_op=ALU.is_gt, fill=0.0,
                                               base=0, pattern=[[1, 128]], channel_multiplier=-1), [c0], "cst")
        k_cst = do("gpsimd", lambda e: e.memset(ones3[0:3, :], 1.0), [c0], "cst")
        k_bz = do("vector", lambda e: e.memset(BS[:, :].bitcast(U32), 0), sig="bz")
        do("vector", lambda e: e.memset(Mb[:, :, :], 0.0), sig="bz")
        do("vector", lambda e: e.memset(OFF[:, 0, :], 0.0), sig="bz")
        do("vector", lambda e: e.memset(pad[:, 0:257], 0.0), sig="bz")
        k_z = do("vector", lambda e: e.memset(pad[:, 257:258].bitcast(I32), T), sig="bz")
        k_idx = do("gpsimd", lambda e: e.iota(ROW[:, :, 257].bitcast(I32), pattern=[[128, NT]], base=0, channel_multiplier=1), [], "idx")

        w = do("vector", lambda e: e.tensor_copy(bsp[:, 0, :], bst[:, 0, :]), [k_b], "bs")
        w = do("vector", lambda e: e.tensor_tensor(bst[:, 1, :], bst[:, 0, :], bsp[:, 0, :], ALU.subtract), [w], "bs")
        w = do("vector", lambda e: e.tensor_copy(bsp[:, 1, :], bst[:, 1, :]), [w], "bs")
        w = do("vector", lambda e: e.tensor_tensor(bst[:, 2, :], bst[:, 1, :], bsp[:, 1, :], ALU.subtract), [w], "bs")
        w = do("vector", lambda e: e.tensor_copy(bsp[:, 2, :], bst[:, 2, :]), [w], "bs")
        w = dma(bsd.rearrange("r (p c) -> p r c", p=128), bsp[:, :, :], [w], "bsd")
        k_bs = dma(BS[0:3, :], bsd, [w, k_bz], "bsr")

        for b in range(1, B):
            k_x.append(dma(ROW[:, 4 * b:4 * b + 4, 128:256], x_v[:, 4 * b:4 * b + 4, :], sig=f"ld_x{b}"))
        k_g = dma(WG[:, :], a["Wg"], sig="ld_g")
        dma(CS[:, :, :, :], a["cs"], sig="ld_c")
        dma(c8[:, :], a["c8"], sig="ld_c")
        dma(e4[:, :], a["e4"], sig="ld_c")
        k_c = dma(tio[:, :], a["tio"], sig="ld_c")
        for i, n in enumerate(("lq1", "lk1", "lq2", "lk2")):
            k_l = dma(lam[:, i, :], a[n].rearrange("(a n) -> a n", a=1).broadcast_to([128, 8]), sig="ld_lam")
        k_pad = [dma(xs[i][NE * REG:SLOTS, :].rearrange("(t p) c -> p t c", p=128),
                     pad[:, :].rearrange("p (o c) -> p o c", o=1).broadcast_to([128, NE - 1, ROWW]), [k_z], f"pad{i}")
                 for i in range(2)]

        def bias(name, lo=0, n=None):
            o, length = BIAS[name]
            return BS[:, o + lo:o + lo + (n or length)]

        def lambdas():
            w = do("vector", lambda e: e.tensor_tensor(lam[:, 0:3:2, :], lam[:, 0:3:2, :], lam[:, 1:4:2, :], ALU.mult), [k_l], "lam")
            w = do("vector", lambda e: e.tensor_reduce(lm[:, 0:2], lam[:, 0:3:2, :], AX, ALU.add), [w], "lam")
            w = do("scalar", lambda e: e.activation(lm[:, 2:4], lm[:, 0:2], ACT.Exp), [w], "lamx")
            w = do("vector", lambda e: e.tensor_tensor(lm[:, 4:5], lm[:, 3:4], lm[:, 2:3], ALU.subtract), [w], "lam")
            return do("vector", lambda e: e.tensor_scalar(lm[:, 5:6], lm[:, 4:5], -(0.8 - 0.6 * float(np.exp(-0.3 * 0))), None, ALU.add),
                      [w], "lam")

        sring = Ring([0, 1, 2])
        oring = Ring([3])
        mring = Ring([4, 5])
        rring = Ring([6, 7])

        def r16(bank):
            return ps[:, bank, :].bitcast(F16)

        ln_last = [None, None]

        def layernorm(b, z, rank, ready):
            t0 = 4 * b
            yield rank, [ready, ln_last[z]]
            for i in range(4):
                w = do("vector", lambda e, i=i: e.bn_stats(st6[:, z, i, :], ROW[:, t0 + i, 128:256]),
                       [ready, ln_last[z]], "lnd")
                if i == 1:
                    yield rank, []
            yield rank, [w]
            for i in range(4):
                w1 = do("vector", lambda e, i=i: e.bn_aggr(mv[:, z, i, :], st6[:, z, i, :]), [w], "lnd", n=8)
            w = do("gpsimd", lambda e: e.tensor_scalar(vs[:, z, :], mv[:, z, :, 1], EPS, None, ALU.add), [w1, k_cst], "lnp", n=4)
            w = do("gpsimd", lambda e: e.tensor_tensor(rs[:, z, :], vs[:, z, :], half[:, :], ALU.pow), [w], "lnp", n=350)
            for i in range(4):
                w2 = do("gpsimd", lambda e, i=i: e.tensor_scalar(ROW[:, t0 + i, 0:128], ROW[:, t0 + i, 128:256],
                                                                mv[:, z, i, 0:1], rs[:, z, i:i + 1], ALU.subtract, ALU.mult),
                        [w], "lnp")
            ln_last[z] = w2
            return w2

        def gate(b, ready, ffn, rank):
            t0 = 4 * b
            hw = yield from layernorm(b, 1, rank, ready)
            ri, bank, free = yield from rring.take(rank, [hw])
            for i in range(4):
                w = do("tensor", lambda e, i=i: e.transpose(ps[:, bank, 128 * i:128 * i + 128], ROW[:, t0 + i, 0:128], idf[:, :]),
                       free + [hw], "g_t" if i == 3 else None, n=256)
            yield rank, [w, att_free[0]]
            wc = do("scalar", lambda e: e.copy(ATT[:, 0, :], ps[:, bank, :]), [w, att_free[0]], "g_c", n=512)
            rring.give(ri, [wc])
            ri, bank2, free = yield from rring.take(rank, [wc])
            o, n = BIAS["bg"]
            do("tensor", lambda e: e.matmul(ps[:, bank2, 0:32], ones3[:, :],
                                            BS[:, o:o + n].rearrange("p (o n) -> p o n", o=1).broadcast_to([128, 4, NE]),
                                            start=True, stop=False, skip_group_check=True), free + [k_bs], n=64)
            for i in range(4):
                w2 = do("tensor", lambda e, i=i: e.matmul(ps[:, bank2, 8 * i:8 * i + 8], ATT[:, 0, 128 * i:128 * i + 128], WG[:, :],
                                                          start=False, stop=(i == 3), skip_group_check=True),
                        [wc, k_g], "g_m" if i == 3 else None, n=256)
            att_free[0] = w2
            yield rank, [w2, gate_free[0]]
            w = do("vector", lambda e: e.tensor_copy(G[:, 0, :], ps[:, bank2, 0:32]), [w2, gate_free[0]], "gd", n=32)
            rring.give(ri, [w])
            lg, dd, ex, vv = (G[:, i, :].rearrange("p (t n) -> p t n", t=4) for i in range(4))

            def bc(x):
                return x.rearrange("p (t o) -> p t o", o=1).broadcast_to([128, 4, NE])

            def row(x):
                return x.rearrange("p (o n) -> p o n", o=1).broadcast_to([128, 4, NE])

            yield rank, [w]
            w = do("vector", lambda e: e.tensor_reduce(g4[:, 0, :], lg, AX, ALU.max), [w], "gd", n=32)
            yield rank, [w]
            wd = do("vector", lambda e: e.tensor_tensor(dd, lg, bc(g4[:, 0, :]), ALU.subtract), [w], "gd", n=32)
            w = do("vector", lambda e: e.tensor_tensor(vv, lg, bc(g4[:, 0, :]), ALU.is_equal), [w], "gd", n=32)
            wx = do("scalar", lambda e: e.activation(ex, dd, ACT.Exp), [wd], "gx", n=32)
            yield rank, [w, k_c]
            w = do("vector", lambda e: e.tensor_tensor(vv, vv, row(c8[:, :]), ALU.mult), [w, k_c], "gd", n=32)
            yield rank, [w]
            w = do("vector", lambda e: e.tensor_reduce(g4[:, 1, :], vv, AX, ALU.max), [w], "gd", n=32)
            oh = OH[:, t0:t0 + 4, :]
            yield rank, [w]
            w = do("vector", lambda e: e.tensor_tensor(oh, row(c8[:, :]), bc(g4[:, 1, :]), ALU.is_equal), [w], "gd", n=32)
            yield rank, [w, wx]
            wo = do("vector", lambda e: e.tensor_copy(OHb[:, :, :], oh), [w], "gd", n=32)
            w = do("vector", lambda e: e.tensor_reduce(g4[:, 2, :], ex, AX, ALU.add), [wx], "gd", n=32)
            yield rank, [w]
            wr = do("vector", lambda e: e.reciprocal(ROW[:, t0:t0 + 4, 256], g4[:, 2, :]), [w], "gd", n=32)
            ri, bank3, free = yield from rring.take(rank, [wo])
            ohf = OHb[:, :, :].rearrange("p t n -> p (t n)")
            do("tensor", lambda e: e.matmul(ps[:, bank3, 0:32], tri[:, :], ohf, start=True, stop=True), free + [wo], n=64)
            w = do("tensor", lambda e: e.matmul(ps[:, bank3, 32:64], ones[:, :], ohf, start=True, stop=True), [], "g_p", n=64)
            for i in range(4):
                yield rank, [w]
                w = do("vector", lambda e, i=i: e.tensor_tensor(OFF[:, t0 + i + 1, :], OFF[:, t0 + i, :],
                                                               ps[:, bank3, 32 + 8 * i:40 + 8 * i], ALU.add), [w], "gd", n=8)
            yield rank, [w]
            w = do("vector", lambda e: e.tensor_tensor(dd, ps[:, bank3, 0:32].rearrange("p (t n) -> p t n", t=4), OFF[:, t0:t0 + 4, :],
                                                       ALU.add), [w], "gd", n=32)
            rring.give(ri, [w])
            yield rank, [w]
            w = do("vector", lambda e: e.tensor_tensor(dd, dd, row(e4[:, :]), ALU.add), [w], "gd", n=32)
            yield rank, [w]
            w = do("vector", lambda e: e.tensor_tensor(dd, dd, oh, ALU.mult), [w], "gd", n=32)
            yield rank, [w]
            w = do("vector", lambda e: e.tensor_reduce(g4[:, 3, :], dd, AX, ALU.add), [w], "gd", n=32)
            yield rank, [w, scat_done[0]]
            w = do("vector", lambda e: e.tensor_copy(slot[:, t0:t0 + 4], g4[:, 3, :]), [w, scat_done[0]], "gd", n=4)
            gate_free[0] = w
            for t in range(t0, t0 + 4):
                do("gpsimd", lambda e, t=t: e.indirect_dma_start(
                    out=xs[ffn][:, :], out_offset=bass.IndirectOffsetOnAxis(ap=slot[:, t:t + 1], axis=0),
                    in_=ROW[:, t, 0:ROWW], in_offset=None), [w, wr, k_idx], f"scat{ffn}", 16, n=380)

        att_free = [None]
        gate_free = [None]
        scat_done = [None]

        LA = dict(n=1, gpb=4, kq=120, ks=124, vw=16, one=8, dv=8, scale=float(1.0 / np.sqrt(40.0)))
        LB = dict(n=2, gpb=8, kq=128, ks=128, vw=20, one=16, dv=16, scale=float(8 ** -0.5))

        def attention(L, x_ready, ffn, first):
            one = L["n"] == 1
            gpb, vw, dv = L["gpb"], L["vw"], L["dv"]
            NG = B * gpb
            name = "a" if one else "b"

            def s(x):
                return f"{name}_{x}"

            if one:
                TQ = TR[:, 0:16384].rearrange("p (u t h c) -> p u t h c", u=2, t=4, c=128)
                TK = TR[:, 16384:32768].rearrange("p (u t h c) -> p u t h c", u=2, t=4, c=128)
                SQ = STK[:, 0:8192].rearrange("p (g j n) -> p g j n", g=4, j=4)
                SK = STK[:, 8192:16384].rearrange("p (g j n) -> p g j n", g=4, j=4)
            else:
                TQ = TR[:, 16384:24576].rearrange("p (u t h c) -> p u t h c", u=2, t=4, c=32)
                TK = TR[:, 24576:32768].rearrange("p (u t h c) -> p u t h c", u=2, t=4, c=32)
                SG = STK[:, 0:4096].rearrange("p (g w n) -> p g w n", g=4, w=2)
                SK = STK[:, 4096:12288].rearrange("p (g j n) -> p g j n", g=4, j=4)

            k_v = do("gpsimd", lambda e: e.memset(V[:, :, :, :], 0.0), first, s("init"))
            Vh = V[:, :, :, 0:16 * vw].rearrange("p u t (h c) -> p (u t) h c", c=vw)
            do("gpsimd", lambda e: e.memset(Vh[:, :, :, L["one"]], 1.0), [k_v], s("init"))
            for u in range(2):
                if one:
                    do("gpsimd", lambda e, u=u: e.memset(TQ[:, u, :, :, 120:128], 0.0), first, s("init"))
                    w = do("gpsimd", lambda e, u=u: e.memset(TK[:, u, :, :, 120:128], 0.0), first, s("init"))
                    for j in range(4):
                        k_i = do("gpsimd", lambda e, u=u, j=j: e.memset(TK[:, u, :, j:16:4, 120 + j], 1.0), [w], s("init"))
                else:
                    w = do("gpsimd", lambda e, u=u: e.memset(TQ[:, u, :, :, 24:32], 0.0), first, s("init"))
                    w = do("gpsimd", lambda e, u=u: e.memset(TK[:, u, :, :, 24:32], 0.0), first, s("init"))
                    k_i = do("gpsimd", lambda e, u=u: e.memset(TK[:, u, :, :, 24], 1.0), [w], s("init"))
            k_sz = None
            if not one:
                k_sz = do("vector", lambda e: e.memset(STK[:, 4096:12288].bitcast(U32), 0), first, s("sz"))

            hready = {}
            split_done = {}
            tp_done = {}
            pv_group = {}
            stack = {}
            mrow = {}
            st_group = {}
            smax_tok = {}
            norm_done = {}
            x_done = {}
            if not one:
                k_lam[0] = lambdas()
            m_read = [None, None]
            mt_read = [None, None]
            or_read = [None, None]
            hT_read = [None] * 4
            rt_read = [None]
            at_read = {}
            rec_read = [None]

            def ln(b):
                while b >= 2 and b - 2 not in proj_done:
                    yield gpb * b - 5, None
                hready[b] = yield from layernorm(b, 0, gpb * b - 5, x_ready[b])

            def proj(b, i):
                u, t, hs = b % 2, 4 * b + i, i % 4
                rank = gpb * b - 4 - (4 - i) * gpb / 4
                while b not in hready or (b > 1 and b - 2 not in tp_done) or (b > 2 and gpb * (b - 2) - 1 not in pv_group):
                    yield rank, None
                tfree = [tp_done.get(b - 2), k_i]
                vfree = [pv_group.get(gpb * (b - 2) - 1), k_i]
                qq, kk = qk_of(u, i)
                ri, bank, free = yield from rring.take(rank, [hready[b]])
                w = do("tensor", lambda e: e.transpose(ps[:, bank, 0:128], ROW[:, t, 0:128], idf[:, :]), free + [hready[b], k_cst],
                       s("ht"), n=256)
                yield rank, [w, hT_read[hs]]
                hw = do("scalar", lambda e: e.copy(HT[:, hs, :], ps[:, bank, 0:128]), [w, hT_read[hs]], s("htc"))
                rring.give(ri, [hw])
                ri, bk, free = yield from rring.take(rank, [hw])
                if one:
                    do("tensor", lambda e: e.matmul(ps[:, bk, :], ones3[:, :], bias("br"), start=True, stop=False), free + [k_bs], n=512)
                    w = do("tensor", lambda e: e.matmul(ps[:, bk, :], HT[:, hs, :], WA[:, 0:512], start=False, stop=True),
                           [hw, k_w1], s("pj"), n=2048)
                    r = ps[:, bk, :].rearrange("p (h c) -> p h c", c=32)
                    r2 = ps[:, bk, :].rearrange("p (h o c) -> p h o c", o=1, c=32).broadcast_to([128, 16, 2, 32])
                    yield rank, [w] + tfree
                    wh = do("scalar", lambda e: e.copy(qq[:, :, 0:64].rearrange("p h (o c) -> p h o c", o=2), r2), [w] + tfree,
                            s("hi"), n=1024)
                    do("gpsimd", lambda e: e.tensor_copy(kk[:, :, 0:32], qq[:, :, 0:32]), [wh], s("cp"), n=700)
                    do("gpsimd", lambda e: e.tensor_copy(kk[:, :, 64:96], qq[:, :, 32:64]), [wh], s("cp"), n=700)
                    yield rank, [wh]
                    wl = do("vector", lambda e: e.tensor_tensor(qq[:, :, 64:96], r, qq[:, :, 0:32], ALU.subtract), [wh], s("lo"), n=512)
                    rring.give(ri, [wl])
                    wc = do("gpsimd", lambda e: e.tensor_copy(kk[:, :, 32:64], qq[:, :, 64:96]), [wl], s("cp"), n=700)
                    ri, bj, free = yield from rring.take(rank)
                    do("tensor", lambda e: e.matmul(ps[:, bj, 0:384], ones3[:, :], bias("bqkv"), start=True, stop=False), free, n=384)
                    w = do("tensor", lambda e: e.matmul(ps[:, bj, 0:384], HT[:, hs, :], WA[:, 512:896], start=False, stop=True),
                           [], s("pj"), n=1536)
                    hT_read[hs] = w
                    qp = ps[:, bj, 0:128]
                    kp = ps[:, bj, 128:256]
                    vp = ps[:, bj, 256:384].rearrange("p (h c) -> p h c", c=8)

                    def two(x):
                        return x.rearrange("p (h o c) -> p h o c", o=1, c=8).broadcast_to([128, 16, 2, 8])

                    k3 = kk[:, :, 96:128].rearrange("p h (o c) -> p h o c", o=4)[:, :, 0:3:2, :]
                    yield rank, [w] + vfree
                    do("scalar", lambda e: e.copy(qq[:, :, 96:112].rearrange("p h (o c) -> p h o c", o=2), two(qp)), [w], s("hi"), n=256)
                    do("scalar", lambda e: e.copy(k3, two(kp)), [], s("hi"), n=256)
                    wh = do("scalar", lambda e: e.copy(V[:, b % 3, i, 0:16 * vw].rearrange("p (h c) -> p h c", c=vw)[:, :, 0:8], vp),
                            vfree, s("hi"))
                    yield rank, [wh]
                    do("vector", lambda e: e.tensor_tensor(qq[:, :, 112:120], qp.rearrange("p (h c) -> p h c", c=8),
                                                           qq[:, :, 96:104], ALU.subtract), [wh], s("lo"))
                    wl = do("vector", lambda e: e.tensor_tensor(kk[:, :, 104:112], kp.rearrange("p (h c) -> p h c", c=8),
                                                                kk[:, :, 96:104], ALU.subtract), [], s("lo"))
                    rring.give(ri, [wl])
                    split_done[b, i] = [wl, wh, wc]
                else:
                    w = do("tensor", lambda e: e.matmul(ps[:, bk, :], HT[:, hs, :], WA[:, 0:512], start=True, stop=True),
                           free + [hw] + k_w2, s("pj"), n=2048)
                    pr = ps[:, bk, :].rearrange("p (x c) -> p x c", c=8)

                    def tab(z):
                        return CS[:, z, i, :].rearrange("p (o c) -> p o c", o=1).broadcast_to([128, 64, 8])

                    yield rank, [w, rt_read[0]]
                    do("vector", lambda e: e.tensor_tensor(RT[:, 0, :].rearrange("p (x c) -> p x c", c=8), pr, tab(0), ALU.mult),
                       [w, rt_read[0], k_c], s("rot"), n=512)
                    yield rank, []
                    wr = do("vector", lambda e: e.tensor_tensor(RT[:, 1, :].rearrange("p (x c) -> p x c", c=8), pr, tab(1), ALU.mult),
                            [], s("rot"), n=512)
                    rring.give(ri, [wr])

                    def part(z, h):
                        return RT[:, z, :].rearrange("p (k h c) -> p k h c", k=2, h=2)[:, :, h, :]

                    do("gpsimd", lambda e: e.tensor_tensor(part(2, 0), part(0, 0), part(1, 1), ALU.subtract), [wr], s("ro2"), n=256)
                    wf = do("gpsimd", lambda e: e.tensor_tensor(part(2, 1), part(0, 1), part(1, 0), ALU.add), [], s("ro2"), n=256)
                    ri, bj, free = yield from rring.take(rank)
                    w = do("tensor", lambda e: e.matmul(ps[:, bj, 0:256], HT[:, hs, :], WA[:, 512:768], start=True, stop=True),
                           free, s("pj"), n=1024)
                    hT_read[hs] = w
                    vo = V[:, b % 3, i, 0:16 * vw].rearrange("p (h c) -> p h c", c=vw)[:, :, 0:16].rearrange("p h (o c) -> p h o c", o=2)
                    vi = ps[:, bj, 0:256].rearrange("p (o h c) -> p h o c", o=2, c=8)
                    yield rank, [w] + vfree
                    wv = do("scalar", lambda e: e.copy(vo, vi), [w] + vfree, s("hi"), n=256)
                    rring.give(ri, [wv])
                    fq, fk = RT[:, 2, 0:256], RT[:, 2, 256:512]

                    def two(x):
                        return x.rearrange("p (h o c) -> p h o c", o=1, c=8).broadcast_to([128, 32, 2, 8])

                    yield rank, [wf] + tfree
                    do("scalar", lambda e: e.copy(qq[:, :, 0:16].rearrange("p h (o c) -> p h o c", o=2), two(fq)), [wf] + tfree,
                       s("hi"), n=512)
                    yield rank, []
                    wh = do("scalar", lambda e: e.copy(kk.rearrange("p h (o c) -> p h o c", o=4)[:, :, 0:3:2, :], two(fk)), [],
                            s("hi"), n=512)
                    do("gpsimd", lambda e: e.tensor_tensor(qq[:, :, 16:24], fq.rearrange("p (h c) -> p h c", c=8), qq[:, :, 0:8],
                                                           ALU.subtract), [wh], s("lo"), n=256)
                    wl = do("gpsimd", lambda e: e.tensor_tensor(kk[:, :, 8:16], fk.rearrange("p (h c) -> p h c", c=8), kk[:, :, 0:8],
                                                                ALU.subtract), [], s("lo"), n=256)
                    rt_read[0] = wl
                    split_done[b, i] = [wl, wh, wv]
                if i == 3:
                    proj_done[b] = True

            def group(g):
                b, gl, sl, rank = g // gpb, g % gpb, g % 4, g - 3.5
                u = b % 2
                while (b, 3) not in split_done or (g >= 4 and g - 4 not in st_group):
                    yield rank, None
                gfree = [st_group.get(g - 4)]
                if one:
                    for i in range(4):
                        yield rank, split_done[b, i] + gfree
                        for T_, S_ in ((TQ, SQ), (TK, SK)):
                            w = do("sync", lambda e, i=i, T_=T_, S_=S_: e.dma_start_transpose(
                                S_[:, sl, :, 128 * i:128 * i + 128], T_[:, u, i, 4 * gl:4 * gl + 4, :].rearrange("p h c -> p (h c)")),
                                split_done[b, i] + gfree, s(f"tp{sl}"), 16, n=1175)
                    stack[g] = [w]
                else:
                    ri, bank, free = yield from rring.take(rank, split_done[b, 3])
                    for z, T_ in ((0, TQ), (1, TK)):
                        for i in range(4):
                            w = do("tensor", lambda e, z=z, i=i, T_=T_: e.transpose(
                                r16(bank)[:, 512 * z + 128 * i:512 * z + 128 * i + 128],
                                T_[:, u, i, 4 * gl:4 * gl + 4, :].rearrange("p h c -> p (h c)"), idh[:, :]),
                                free + split_done[b, i], s("tp") if z + i == 4 else None)
                    yield rank, [w] + gfree
                    w2 = do("scalar", lambda e: e.copy(SG[:, sl], r16(bank).rearrange("p (w n) -> p w n", w=2)), [w] + gfree,
                            s("tpc"), n=1024)
                    rring.give(ri, [w2])
                    for j in range(4):
                        w3 = dma(SK[32 * j:32 * j + 32, sl, j, :], SG[32 * j:32 * j + 32, sl, 1, :], [w2, k_sz], s(f"msk{sl}"))
                    stack[g] = [w2, w3]
                if gl == gpb - 1:
                    tp_done[b] = w

            def smax(g, qt, j):
                sl, c = g % 4, 4 * qt + j
                while g not in stack or (g >= 2 and g - 2 not in mrow):
                    yield g - 2, None
                ri, bank, free = yield from mring.take(g - 2 + c / 16, stack[g])
                if one:
                    l_, r_ = SQ[0:120, sl, j, 128 * qt:128 * qt + 128], SK[0:120, sl, j, :]
                else:
                    l_, r_ = SG[:, sl, 0, 128 * qt:128 * qt + 128], SK[:, sl, j, :]
                w = do("tensor", lambda e: e.matmul(ps[:, bank, :], l_, r_, start=True, stop=True), free + stack[g], s("sm"), n=512)
                w2 = do("vector", lambda e: e.tensor_reduce(Mb[:, g % 2, 32 * qt + j:32 * qt + j + 1], ps[:, bank, :], AX, ALU.max),
                        [w, m_read[g % 2]], s("mx"), n=512)
                mring.give(ri, [w2])
                if c == 15:
                    smax_tok[g] = (w, w2)

            def mrows(g):
                sl, z, rank = g % 4, g % 2, g - 1.5
                while g not in smax_tok:
                    yield rank, None
                ri, bank, free = yield from rring.take(rank, [smax_tok[g][1]])
                w = do("tensor", lambda e: e.transpose(ps[:, bank, 0:128], Mb[:, z, :], idf[:, :]), free + [smax_tok[g][1]],
                       s("mt"), n=256)
                m_read[z] = w
                yield rank, [w, mt_read[z]]
                w2 = do("scalar", lambda e: e.mul(Mt[:, z, :], ps[:, bank, 0:128], -1.0), [w, mt_read[z]], s("mc"))
                rring.give(ri, [w2])
                for qt in range(4):
                    src = Mt[32 * qt:32 * qt + 4, z, :]
                    if one:
                        dst = SQ[120:124, sl, :, 128 * qt:128 * qt + 128]
                        src = src.rearrange("p (o n) -> p o n", o=1).broadcast_to([4, 4, 128])
                    else:
                        dst = SG[24:128:32, sl, 0, 128 * qt:128 * qt + 128]
                    w3 = dma(dst, src, [w2, smax_tok[g][0]], s(f"mr{sl}"))
                mt_read[z] = w3
                mrow[g] = w3

            def scores(st, j):
                g, kt, sl, z = st // 4, st % 4, st // 4 % 4, st % 2
                rank = g + kt / 4 + j / 16
                while g not in mrow or (st >= 2 and st - 2 not in pv_tok):
                    yield rank, None
                si, bank, free = yield from sring.take(rank, [mrow[g]])
                if one:
                    l_, r_ = SK[0:124, sl, j, 128 * kt:128 * kt + 128], SQ[0:124, sl, j, :]
                else:
                    l_, r_ = SK[:, sl, j, 128 * kt:128 * kt + 128], SG[:, sl, 0, :]
                w = do("tensor", lambda e: e.matmul(ps[:, bank, :], l_, r_, start=True, stop=True), free + [mrow[g]], s("st"), n=512)
                w2 = do("scalar", lambda e: e.activation(P[:, z, j, :], ps[:, bank, :], ACT.Exp, scale=L["scale"]),
                        [w, pv_tok.get(st - 2)], s("exp"), n=512)
                sring.give(si, [w2])
                if j == 3:
                    exp_tok[st] = w2
                    if kt == 3:
                        st_group[g] = w

            def pv(st):
                g, kt = st // 4, st % 4
                b, hh, rank = g // gpb, (g % gpb) % 4, st / 4 + 0.3
                while st not in exp_tok:
                    yield rank, None
                if kt == 0:
                    o_use[g] = yield from oring.take(rank, [exp_tok[st]])
                else:
                    yield rank, [exp_tok[st]]
                oi, bank, free = o_use[g]
                for j in range(4):
                    h = 4 * hh + j
                    w = do("tensor", lambda e, j=j, h=h: e.matmul(ps[32 * j:32 * j + 32, bank, :], V[:, b % 3, kt, vw * h:vw * h + 32],
                                                                  P[:, st % 2, j, :], start=(kt == 0), stop=(kt == 3)),
                           (free if kt == 0 else []) + [exp_tok[st]] + split_done[b, 3], s("pv") if j == 3 else None, n=510)
                pv_tok[st] = w
                if kt == 3:
                    pv_group[g] = w

            def norm(g):
                z, gl, b, rank = g % 2, g % gpb, g // gpb, g + 1
                hh = gl % 4
                while g not in pv_group:
                    yield rank, None
                yield rank, [pv_group[g], or_read[z]]
                oi, bank, _ = o_use[g]
                w = do("scalar", lambda e: e.copy(OR[:, z, :], ps[:, bank, :]), [pv_group[g], or_read[z]], s("oc"), n=512)
                oring.give(oi, [w])
                rank = g + 1.5
                while b and b - 1 not in at_read:
                    yield rank, None
                ri, rb, free = yield from rring.take(rank, [w])
                for i in range(4):
                    w1 = do("tensor", lambda e, i=i: e.transpose(ps[:, rb, 128 * i:128 * i + 128], OR[:, z, 128 * i:128 * i + 128], idf[:, :]),
                            free + [w], s("ot") if i == 3 else None, n=256)
                or_read[z] = w1
                o4 = ps[:, rb, :].rearrange("p (t j c) -> p t j c", t=4, j=4)
                rc = rec[:, 0, :].rearrange("p (t j) -> p t j", t=4)
                yield rank, [w1]
                w2 = do("vector", lambda e: e.reciprocal(rc, o4[:, :, :, L["one"]]), [w1, rec_read[0]], s("nm"))
                yield rank, [w2]
                c0 = hh * 4 * dv
                ao = AT[:, :, c0:c0 + 4 * dv].rearrange("p t (j c) -> p t j c", j=4)
                if gl < 4:
                    rb4 = rec[:, 0, :].rearrange("p (t j o) -> p t j o", t=4, o=1).broadcast_to([128, 4, 4, dv])
                    w3 = do("vector", lambda e: e.tensor_tensor(ao, o4[:, :, :, 0:dv], rb4, ALU.mult), [w2, at_read.get(b - 1)],
                            s("nm"), n=16 * dv)
                    rring.give(ri, [w3])
                else:
                    w3 = do("vector", lambda e: e.tensor_scalar(rec[:, 1, :], rec[:, 0, :], lm[:, 5:6], None, ALU.mult),
                            [w2, k_lam[0]], s("nm"), n=16)
                    yield rank, [w3]
                    rb4 = rec[:, 1, :].rearrange("p (t j o) -> p t j o", t=4, o=1).broadcast_to([128, 4, 4, dv])
                    tmp = OT[:, :].rearrange("p (t j c) -> p t j c", t=4, j=4)
                    w3 = do("vector", lambda e: e.tensor_tensor(tmp, o4[:, :, :, 0:dv], rb4, ALU.mult), [w3], s("nm"), n=256)
                    rring.give(ri, [w3])
                    yield rank, [w3]
                    w3 = do("vector", lambda e: e.tensor_tensor(ao, ao, tmp, ALU.add), [w3], s("nm"), n=256)
                rec_read[0] = w3
                norm_done[g] = w3

            def out(b):
                rank = gpb * (b + 1) + 2
                while gpb * (b + 1) - 1 not in norm_done:
                    yield rank, None
                nd = norm_done[gpb * (b + 1) - 1]
                for c in range(1 if one else 2):
                    ri, bank, free = yield from rring.take(rank, [nd])
                    for i in range(4):
                        w = do("tensor", lambda e, i=i, c=c, bank=bank: e.transpose(ps[:, bank, 128 * i:128 * i + 128],
                                                                                    AT[:, i, 128 * c:128 * c + 128], idf[:, :]),
                               free + [nd], s("at") if i == 3 else None, n=256)
                    yield rank, [w, att_free[0]]
                    w2 = do("scalar", lambda e, c=c, bank=bank: e.copy(ATT[:, c, :], ps[:, bank, :]), [w, att_free[0]], s("atc"), n=512)
                    rring.give(ri, [w2])
                at_read[b] = w
                ri, bank, free = yield from rring.take(rank, [w2])
                if one:
                    o, n = BIAS["bo"]
                    do("tensor", lambda e: e.matmul(ps[:, bank, :], ones3[:, :],
                                                    BS[:, o:o + n].rearrange("p (o n) -> p o n", o=1).broadcast_to([128, 4, 128]),
                                                    start=True, stop=False, skip_group_check=True), free, n=512)
                    for i in range(4):
                        w = do("tensor", lambda e, i=i: e.matmul(ps[:, bank, 128 * i:128 * i + 128], ATT[:, 0, 128 * i:128 * i + 128],
                                                                 WA[:, 896:1024], start=False, stop=(i == 3), skip_group_check=True),
                               [w2], s("op") if i == 3 else None, n=512)
                else:
                    for i in range(4):
                        for c in range(2):
                            w = do("tensor", lambda e, i=i, c=c: e.matmul(ps[:, bank, 128 * i:128 * i + 128],
                                                                          ATT[:, c, 128 * i:128 * i + 128],
                                                                          WA[:, 768 + 128 * c:896 + 128 * c], start=(c == 0), stop=(c == 1)),
                                   free + [w2], s("op") if i == 3 and c == 1 else None, n=512)
                att_free[0] = w
                xr = ROW[:, 4 * b:4 * b + 4, 128:256]
                yield rank, [w]
                w = do("vector", lambda e: e.tensor_tensor(xr, xr, ps[:, bank, :].rearrange("p (t n) -> p t n", t=4), ALU.add),
                       [w], s("res"), n=512)
                rring.give(ri, [w])
                yield from gate(b, w, ffn, rank + 1)

            exp_tok, pv_tok, o_use, proj_done = {}, {}, {}, {}

            def qk_of(u, i):
                return TQ[:, u, i], TK[:, u, i]

            def each(stage, *counts):
                for i in np.ndindex(*counts):
                    yield from stage(*i)

            q.run([each(scores, 4 * NG, 4), each(pv, 4 * NG), each(smax, NG, 4, 4), each(mrows, NG), each(norm, NG),
                   each(group, NG), each(proj, B, 4), each(ln, B), each(out, B)])
            return x_done

        OT = sb("OT", [128, 256], F32)
        k_w2 = []
        k_lam = [None]

        def experts(n, dst):
            Cn = OFF[:, NT, :]
            w0 = gate_free[0]
            wp = do("vector", lambda e: e.tensor_tensor(ri[:, FT:FT + NE], Cn, e4[:, :], ALU.add), [w0], "rt")
            w = do("vector", lambda e: e.tensor_scalar(E8i[:, 0, :], Cn, 127.0, None, ALU.add), [w0], "rt")
            w = do("vector", lambda e: e.tensor_scalar(E8i[:, 1, :], E8i[:, 0, :], 7, None, ALU.logical_shift_right), [w], "rt")
            w = do("vector", lambda e: e.tensor_copy(E8[:, 0, :], E8i[:, 1, :]), [w], "rt")
            wn = do("vector", lambda e: e.tensor_scalar(E8[:, 3, :], E8[:, 0, :], -128.0, float(REG), ALU.mult, ALU.add), [w], "rt")
            at = 0
            for k in (1, 2, 4):
                to = 1 if at != 1 else 2
                do("vector", lambda e, k=k, at=at, to=to: e.tensor_copy(E8[:, to, 0:k], E8[:, at, 0:k]), [w], "rt")
                w = do("vector", lambda e, k=k, at=at, to=to: e.tensor_tensor(E8[:, to, k:NE], E8[:, at, k:NE], E8[:, at, 0:NE - k],
                                                                              ALU.add), [w], "rt")
                at = to
            cmp = RT[:, 2, 0:FT * NE].rearrange("p (t n) -> p t n", n=NE)
            tb = tio[:, :].rearrange("p (t o) -> p t o", o=1).broadcast_to([128, FT, NE])

            def each(x):
                return x.rearrange("p (o n) -> p o n", o=1).broadcast_to([128, FT, NE])

            w = do("vector", lambda e: e.tensor_tensor(cmp, each(E8[:, at, :]), tb, ALU.is_le), [w, k_c], "rt")
            w1 = do("vector", lambda e: e.tensor_reduce(ef[:, 0, :], cmp, AX, ALU.add), [w], "rt")
            w2 = do("vector", lambda e: e.tensor_tensor(cmp, cmp, each(E8[:, 3, :]), ALU.mult), [w1, wn], "rt")
            w1 = do("vector", lambda e: e.tensor_scalar(ef[:, 1, :], ef[:, 0, :], float(NE - 1), None, ALU.min), [w1], "rt")
            w2 = do("vector", lambda e: e.tensor_reduce(ef[:, 2, :], cmp, AX, ALU.add), [w2], "rt")
            w1 = do("vector", lambda e: e.tensor_scalar(eoff[:, 0, :], ef[:, 1, :], float(FH), None, ALU.mult), [w1], "rt")
            w2 = do("vector", lambda e: e.scalar_tensor_tensor(out=ri[:, 0:FT], in0=tio[:, :], scalar=128.0, in1=ef[:, 2, :],
                                                               op0=ALU.mult, op1=ALU.add), [w2], "rt")
            we = do("vector", lambda e: e.tensor_scalar(eoff[:, 1, :], ef[:, 1, :], float(D), None, ALU.mult), [w1], "rt")
            w_sc = q.last(f"scat{n}")
            scat_done[0] = w_sc

            for k in range(NE):
                def fill(e, k=k):
                    v = e.value_load(ri[0:1, FT + k:FT + k + 1], min_val=k * REG, max_val=k * REG + T)
                    return e.dma_start(xs[n][bass.ds(v, 128), :], pad[:, :])

                w_pad = do("sync", fill, [wp, k_z], f"fill{n}", 16)

            W1 = TR[:, 0:8192].bitcast(F32)
            W2 = TR[:, 8192:16384].bitcast(F32)
            if n == 0:
                k_e[0] = [dma(W1[:, :], a["W1"], ffn_first, "ld_w1", engine="scalar"),
                          dma(W2[:, :], a["W2"], [], "ld_w2", engine="scalar")]
                dma(WA[:, 0:768], a["Wqkv"], ffn_first, "ld_wb", engine="scalar")
                k_w2.append(dma(WA[:, 768:1024].rearrange("p (c n) -> p c n", c=2), a["Wproj"], [], "ld_wb", engine="scalar"))

            fP = P[:, :, :, :].rearrange("p z j n -> p (z j n)")
            X = [STK[:, 520 * i:520 * i + 516].bitcast(F32) for i in range(6)]
            XT = [STK[:, 4096 + 256 * i:4352 + 256 * i].bitcast(F32) for i in range(3)]
            Y = [STK[:, 5120 + 256 * i:5376 + 256 * i].bitcast(F32) for i in range(6)]
            A = [fP[:, 512 * i:512 * i + 512] for i in range(3)]
            A2 = [fP[:, 2048 + 512 * i:2560 + 512 * i] for i in range(3)]
            ring = Ring([0, 1, 2, 3, 4, 5, 6, 7])
            ld, xt_r, a_r, a2_r, yy, sc, regs = {}, {}, {}, {}, {}, {}, {}

            def load(t):
                def fetch(e):
                    v = e.value_load(ri[0:1, t:t + 1], min_val=0, max_val=SLOTS - 128)
                    return e.dma_start(X[t % 6], xs[n][bass.ds(v, 128), :])

                ld[t] = do("sync", fetch, [w_sc, w2, w_pad, k_pad[n], sc.get(t - 6), yy.get(t - 6)] + ffn_first, f"ldx{t % 6}", 16, n=800)

            def offsets(t):
                def go(e):
                    regs[t] = (e.value_load(eoff[0:1, 0, t:t + 1], min_val=0, max_val=(NE - 1) * FH),
                               e.value_load(eoff[0:1, 1, t:t + 1], min_val=0, max_val=(NE - 1) * D))

                do("tensor", go, [we], n=64)

            def block(t):
                while t > 5 and t - 6 not in sc:
                    yield t, None
                load(t)
                while t > 2 and t - 3 not in xt_r:
                    yield t, None
                ri_, bank, free = yield from ring.take(t, [ld[t]])
                w = do("tensor", lambda e: e.transpose(ps[:, bank, 0:128], X[t % 6][:, 0:128], idf[:, :]), free + [ld[t]], "f_t", n=256)
                yield t, [w, xt_r.get(t - 3)]
                xt = do("vector", lambda e: e.tensor_copy(XT[t % 3], ps[:, bank, 0:128]), [w, xt_r.get(t - 3)], "f_d")
                ring.give(ri_, [xt])
                while t > 2 and t - 3 not in a_r:
                    yield t, None
                ri_, bank2, free = yield from ring.take(t, [xt])

                def up(e):
                    v = regs[t][0]
                    o = BIAS["b1"][0]
                    e.matmul(ps[:, bank2, :], ones3[:, :], BS[:, bass.ds(v + o, FH)], start=True, stop=False)
                    return e.matmul(ps[:, bank2, :], XT[t % 3], W1[:, bass.ds(v, FH)], start=False, stop=True)

                w = do("tensor", up, free + [xt, we] + k_e[0], "f_u", n=2560)
                xt_r[t] = w
                if t + 1 < FT:
                    offsets(t + 1)
                yield t, [w, a_r.get(t - 3)]
                act = do("scalar", lambda e: e.activation(A[t % 3], ps[:, bank2, :], ACT.Silu), [w, a_r.get(t - 3)] + ffn_first, "f_s", n=512)
                ring.give(ri_, [act])
                while t > 2 and t - 3 not in a2_r:
                    yield t, None
                ri_, bank4, free = yield from ring.take(t, [act])
                for c in range(4):
                    w = do("tensor", lambda e, c=c: e.transpose(ps[:, bank4, 128 * c:128 * c + 128], A[t % 3][:, 128 * c:128 * c + 128], idf[:, :]),
                           free + [act], "f_at" if c == 3 else None, n=256)
                a_r[t] = w
                yield t, [w, a2_r.get(t - 3)]
                act2 = do("vector", lambda e: e.tensor_copy(A2[t % 3], ps[:, bank4, :]), [w, a2_r.get(t - 3)] + ffn_first, "f_d", n=512)
                ring.give(ri_, [act2])
                ri_, bank3, free = yield from ring.take(t, [act2])

                def down(e):
                    v, v2 = regs[t]
                    o = BIAS["b2"][0]
                    e.matmul(ps[:, bank3, 0:128], ones3[:, :], BS[:, bass.ds(v2 + o, D)], start=True, stop=False)
                    for c in range(4):
                        m = e.matmul(ps[:, bank3, 0:128], A2[t % 3][:, 128 * c:128 * c + 128], W2[:, bass.ds(v + 128 * c, D)],
                                     start=False, stop=(c == 3))
                    return m

                w = do("tensor", down, free + [act2], "f_o", n=2200)
                a2_r[t] = w
                yield t, [w]
                yy[t] = do("vector", lambda e: e.scalar_tensor_tensor(out=Y[t % 6], in0=ps[:, bank3, 0:128], scalar=X[t % 6][:, 256:257],
                                                                      in1=X[t % 6][:, 128:256], op0=ALU.mult, op1=ALU.add),
                           [w, sc.get(t - 6)], "f_d")
                ring.give(ri_, [yy[t]])
                sc[t] = do("gpsimd", lambda e: e.indirect_dma_start(
                    out=dst[:, :], out_offset=bass.IndirectOffsetOnAxis(ap=X[t % 6][:, 257:258].bitcast(U32), axis=0),
                    in_=Y[t % 6], in_offset=None, bounds_check=T - 1, oob_is_err=False), [yy[t]], f"so{n}_{t % 6}", 16, n=380)

            offsets(0)
            q.run([block(t) for t in range(FT)])
            for r in (sring, oring, mring, rring):
                r.free = [ring.free[i] for i in r.banks]
            return [sc[t] for t in range(FT - 6, FT)], [q.last("f_o"), q.last("f_d"), q.last("f_s")]

        k_e = [None]
        ffn_first = []
        x1 = attention(LA, k_x, 0, [])
        ffn_first = [q.last("a_st"), q.last("a_pv"), *(q.last(f"a_tp{i}") for i in range(4)), q.last("a_op"), q.last("a_exp"), q.last("a_pj"), q.last("a_sm")]
        end0, rest0 = experts(0, x2)
        x2_v = x2.rearrange("(t p) d -> p t d", p=128)
        k_x2 = []
        for b in range(B):
            k_x2.append(dma(ROW[:, 4 * b:4 * b + 4, 128:256], x2_v[:, 4 * b:4 * b + 4, :], end0, f"ld_xx{b}"))
        x3 = attention(LB, k_x2, 1, ffn_first + rest0 + end0)
        ffn_first = [q.last("b_st"), q.last("b_pv"), q.last("b_tp"), q.last("b_op"), q.last("b_exp"), q.last("b_pj"), q.last("b_sm")]
        end1, _ = experts(1, a["out"])
        do("gpsimd", None, end1)

        block = ctx.enter_context(nc.Block())

        @block.sync
        def _(eng):
            q.play("sync", eng)

        @block.gpsimd
        def _(eng):
            q.play("gpsimd", eng)

        @block.scalar
        def _(eng):
            q.play("scalar", eng)

        @block.vector
        def _(eng):
            q.play("vector", eng)

        @block.tensor
        def _(eng):
            q.play("tensor", eng)


def tables():
    inv = (np.float32(1.0) / np.power(np.float32(10000.0), np.arange(0, 16, 2, dtype=np.float32) / np.float32(16))).astype(np.float32)
    f = (np.arange(S, dtype=np.float32)[:, None] * inv[None, :]).astype(np.float32)
    cs = np.stack([np.cos(f), np.sin(f)]).astype(np.float32)
    cs = np.ascontiguousarray(cs.reshape(2, 4, 128, 8).transpose(2, 0, 1, 3))
    c8 = np.tile(np.arange(NE, 0, -1, dtype=np.float32), (128, 1))
    tio = np.tile(np.arange(FT, dtype=np.float32), (128, 1))
    e4 = np.tile(np.arange(NE, dtype=np.float32) * REG, (128, 1))
    return cs, c8, e4, tio


def kernel(**inputs):
    import concourse.bacc as bacc
    from concourse.bass_utils import run_bass_kernel_spmd

    i = {k: np.asarray(v) for k, v in inputs.items()}
    pa, pb, pf = "L0_attn_a_", "L0_attn_b_", "L0_ffn_"
    cs, c8, e4, tio = tables()
    bias = np.concatenate([i[pa + "br"], i[pa + "bq"], i[pa + "bk"], i[pa + "bv"], i[pa + "bo"], i[pf + "bg"],
                           i[pf + "b1"].reshape(-1), i[pf + "b2"].reshape(-1)])
    bias = np.concatenate([bias, np.zeros(BIASW * 128 - bias.shape[0], bias.dtype)])
    arrays = {
        "x": i[pa + "x"].reshape(T, D), "Wq": i[pa + "Wq"], "Wk": i[pa + "Wk"], "Wv": i[pa + "Wv"], "Wr": i[pa + "Wr"],
        "Wo": i[pa + "Wo"], "bias": bias, "Wg": i[pf + "Wg"],
        "W1": i[pf + "W1"].transpose(1, 0, 2).reshape(D, NE * FH),
        "W2": i[pf + "W2"].reshape(NE, 4, 128, D).transpose(2, 0, 1, 3).reshape(128, NE * 4 * D),
        "Wqkv": i[pb + "W_qkv"].T, "Wproj": i[pb + "W_proj"].T.reshape(2, 128, D).transpose(1, 0, 2),
        "lq1": i[pb + "lambda_q1"], "lk1": i[pb + "lambda_k1"], "lq2": i[pb + "lambda_q2"], "lk2": i[pb + "lambda_k2"],
        "cs": cs, "c8": c8, "e4": e4, "tio": tio,
    }
    arrays = {f"in_{k}": np.ascontiguousarray(v) for k, v in arrays.items()}
    nc = bacc.Bacc("TRN2", target_bir_lowering=False, num_devices=1)
    aps = {k[3:]: nc.dram_tensor(k, v.shape, mybir.dt.from_np(v.dtype), kind="ExternalInput").ap() for k, v in arrays.items()}
    aps["out"] = nc.dram_tensor("out0", (T, D), F32, kind="ExternalOutput").ap()
    build(nc, aps)
    r = run_bass_kernel_spmd(nc, [arrays], core_ids=[0])
    return r.results[0]["out0"].reshape(B, S, D)
```

```python
from contextlib import ExitStack

import numpy as np

import concourse.bass as bass
from concourse import mybir

F32 = mybir.dt.float32
F16 = mybir.dt.float16
BF16 = mybir.dt.bfloat16
I32 = mybir.dt.int32
U32 = mybir.dt.uint32
ALU = mybir.AluOpType
ACT = mybir.ActivationFunctionType
AX = mybir.AxisListType.X

B = 8
S = 512
D = 128
T = B * S
NT = T // 128
NE = 8
FH = 512
FT = 4 * 7 + NE - 1
REG = 7 * S + 128
ROWW = 259
EPS = 1e-5
WEW = FH + 4 + 4 * D + D
BIAS = {"br": (0, 512), "bqkv": (512, 384), "bo": (896, 128), "bg": (1024, 8)}
BIASW = 9
NB = 2 * B
NG = 4 * B + 8 * B
SEGS = [(0, 3), (3, 8), (8, 15), (15, 16)]
HOLD = [False, False, False, True]
SEG_RANK = [(19.77, 0.27), (32.89, 0.34), (78.80, 0.41), (100.00, 0.10)]
EARLY = 60


class Queues:

    PRICE = {"tensor": (4, 0.42), "vector": (65, 1.05), "scalar": (55, 0.83), "gpsimd": (100, 2.5), "sync": (0, 1.0)}
    SIGNAL = {"tensor": 200, "vector": 160, "scalar": 195, "gpsimd": 180}
    DMA = {"sync": 1900, "scalar": 1900, "gpsimd": 3500}

    def __init__(self, sem):
        self.sem = sem
        self.count = {}
        self.lists = {"tensor": [], "vector": [], "scalar": [], "gpsimd": [], "sync": []}
        self.clock = {e: 0.0 for e in self.lists}
        self.due = {}

    def do(self, engine, make, waits=(), sig=None, inc=1, n=128):
        waits = [w for w in waits if w is not None]
        self.lists[engine].append((make, waits, sig, inc))
        fixed, each = self.PRICE[engine]
        self.clock[engine] = max(self.clock[engine], self.when(waits)) + fixed + each * n
        if sig is None:
            return None
        self.count[sig] = self.count.get(sig, 0) + inc
        self.due[sig, self.count[sig]] = self.clock[engine] + (self.DMA[engine] if inc == 16 else self.SIGNAL[engine])
        return (sig, self.count[sig])

    def when(self, tokens):
        return max((self.due[t] for t in tokens if t is not None), default=0.0)

    def last(self, sig):
        return (sig, self.count[sig])

    def run(self, streams):
        heads = [[s, h] for s, h in ((s, next(s, None)) for s in streams) if h is not None]
        while heads:
            best = None
            for i, (s, h) in enumerate(heads):
                if h[1] is None:
                    h = heads[i][1] = next(s, None)
                    if h is None:
                        best = None
                        break
                if h[1] is not None:
                    key = (max(self.clock["tensor"], self.when(h[1])), h[0])
                    if best is None or key < best[0]:
                        best = (key, i)
            else:
                if best is None:
                    raise RuntimeError("no stage can be queued")
                i = best[1]
                heads[i][1] = next(heads[i][0], None)
            if heads[i][1] is None:
                heads.pop(i)

    def play(self, engine, eng):
        seen = {}
        for make, waits, sig, inc in self.lists[engine]:
            for name, value in waits:
                if seen.get(name, 0) < value:
                    eng.wait_ge(self.sem(name), value)
                    seen[name] = value
            if make is None:
                continue
            ins = make(eng)
            if sig is not None:
                ins.then_inc(self.sem(sig), inc)


class Ring:

    def __init__(self, banks):
        self.banks = banks
        self.free = [[] for _ in banks]
        self.idle = list(range(len(banks)))

    def take(self, rank, waits=()):
        waits = list(waits)
        while True:
            if not self.idle:
                yield rank, None
                continue
            i = self.idle[0]
            yield rank, self.free[i] + waits
            if self.idle and self.idle[0] == i:
                self.idle.pop(0)
                return i, self.banks[i], list(self.free[i])

    def give(self, i, tokens):
        self.free[i] = tokens
        self.idle.append(i)


def build(nc, a):
    with ExitStack() as ctx:
        def sb(name, shape, dt):
            return ctx.enter_context(nc.sbuf_tensor(name, shape, dt))

        sems = {}

        def sem(name):
            if name not in sems:
                sems[name] = ctx.enter_context(nc.semaphore(name))
            return sems[name]

        q = Queues(sem)
        do = q.do

        ps = ctx.enter_context(nc.psum_tensor("ps", [128, 8, 512], F32))
        ROW = sb("ROW", [128, 16, ROWW], F32)
        TR = sb("TR", [128, 32768], F16)
        STK = sb("STK", [128, 16384], F16)
        V = sb("V", [128, 3, 4, 336], F32)
        P = sb("P", [128, 3, 4, 512], F32)
        BS = sb("BS", [128, BIASW * 128], BF16)
        OR = sb("OR", [128, 512], F32)
        AT = sb("AT", [128, 4, 256], F32)
        ATT = sb("ATT", [128, 2, 512], F32)
        HT = sb("HT", [128, 2, 128], F32)
        WA = sb("WA", [128, 1024], F32)
        WG = sb("WG", [128, NE], F32)
        CS = sb("CS", [128, 2, 4, 8], F32)
        idf = sb("idf", [128, 128], F32)
        ones = sb("ones", [128, 128], BF16)
        ones3 = sb("ones3", [128, 128], BF16)
        tri = sb("tri", [128, 128], BF16)
        Mb = sb("Mb", [128, 2, 128], F32)
        Mt = sb("Mt", [128, 2, 128], F16)
        st6 = sb("st6", [128, 2, 4, 6], F32)
        mv = sb("mv", [128, 2, 4, 2], F32)
        rs = sb("rs", [128, 2, 4], F32)
        vs = sb("vs", [128, 2, 4], F32)
        half = sb("half", [128, 4], F32)
        rec = sb("rec", [128, 2, 16], F32)
        c8 = sb("c8", [128, NE], F32)
        e4 = sb("e4", [128, NE], F32)
        e127 = sb("e127", [128, NE], F32)
        tio = sb("tio", [128, FT], F32)
        G = sb("G", [128, 3, 32], F32)
        g4 = sb("g4", [128, 5, 4], F32)
        OH = sb("OH", [128, 4, NE], F32)
        OHb = sb("OHb", [128, 4, NE], BF16)
        OFF = sb("OFF", [128, 2, 2, NE], F32)
        E8 = sb("E8", [128, 4, NE], F32)
        E8i = sb("E8i", [128, 2, NE], I32)
        slot = sb("slot", [128, 16], U32)
        cmp = sb("cmp", [128, FT, NE], F32)
        ef = sb("ef", [128, 4, FT], F32)
        ri = sb("ri", [128, 2, 2 * FT + NE], I32)
        lam = sb("lam", [128, 4, 8], F32)
        lm = sb("lm", [128, 6], F32)
        bst = sb("bst", [128, 3, BIASW], F32)
        bsp = sb("bsp", [128, 3, BIASW], BF16)
        pad = sb("pad", [128, ROWW], F32)
        X = sb("X", [128, 6, ROWW], F32)
        XT = sb("XT", [128, 2, 128], F32)
        WE = sb("WE", [128, 3, WEW], F32)
        Z = sb("Z", [128, 2, 512], F32)
        TH = sb("TH", [128, 2, 512], F32)

        xs = [nc.dram_tensor(f"xs{i}", [NE * REG + 128, ROWW], F32, kind="Internal").ap() for i in range(len(SEGS))]
        x2 = nc.dram_tensor("x2", [T, D], F32, kind="Internal").ap()
        bsd = nc.dram_tensor("bsd", [3, BIASW * 128], BF16, kind="Internal").ap()
        x_v = a["x"].rearrange("(t p) d -> p t d", p=128)
        x2_v = x2.rearrange("(t p) d -> p t d", p=128)

        def dma(out, in_, waits=(), sig=None, engine="sync", n=650):
            return do(engine, lambda e: e.dma_start(out, in_), waits, sig, 16, n)

        x_ld = {0: dma(ROW[:, 0:4, 128:256], x_v[:, 0:4, :], sig="ld_x0")}
        k_b = dma(bst[:, 0, :], a["bias"].rearrange("(p c) -> p c", p=128), sig="ld_bias")
        k_w1 = dma(WA[:, 0:512], a["Wr"], sig="ld_wa")
        for i, n in enumerate(("Wq", "Wk", "Wv", "Wo")):
            k_w1 = dma(WA[:, 512 + 128 * i:640 + 128 * i], a[n], sig="ld_wa")
        do("gpsimd", lambda e: e.memset(idf[:, :], 0.0), sig="cst")
        do("gpsimd", lambda e: e.memset(half[:, :], -0.5), sig="cst")
        c0 = do("gpsimd", lambda e: e.memset(ones3[:, :], 0.0), sig="cst")
        do("gpsimd", lambda e: e.affine_select(out=idf[:, :], in_=idf[:, :], compare_op=ALU.not_equal, fill=1.0, base=0,
                                               pattern=[[-1, 128]], channel_multiplier=1), [c0], "cst")
        k_cst = do("gpsimd", lambda e: e.memset(ones3[0:3, :], 1.0), [c0], "cst")
        k_bz = do("vector", lambda e: e.memset(BS[:, :].bitcast(U32), 0), sig="bz")
        do("vector", lambda e: e.memset(Mb[:, :, :], 0.0), sig="bz")
        do("vector", lambda e: e.memset(pad[:, :], 0.0), sig="bz")
        k_z = do("vector", lambda e: e.memset(pad[:, 257:258].bitcast(I32), T), [q.last("bz")], sig="bz")

        w = do("vector", lambda e: e.tensor_copy(bsp[:, 0, :], bst[:, 0, :]), [k_b], "bs", n=8)
        w = do("vector", lambda e: e.tensor_tensor(bst[:, 1, :], bst[:, 0, :], bsp[:, 0, :], ALU.subtract), [w], "bs", n=8)
        w = do("vector", lambda e: e.tensor_copy(bsp[:, 1, :], bst[:, 1, :]), [w], "bs", n=8)
        w = do("vector", lambda e: e.tensor_tensor(bst[:, 2, :], bst[:, 1, :], bsp[:, 1, :], ALU.subtract), [w], "bs", n=8)
        w = do("vector", lambda e: e.tensor_copy(bsp[:, 2, :], bst[:, 2, :]), [w], "bs", n=8)
        w = dma(bsd.rearrange("r (p c) -> p r c", p=128), bsp[:, :, :], [w], "bsd")
        k_bs = dma(BS[0:3, :], bsd, [w, k_bz], "bsr")

        def later():
            k = {}
            for b in range(1, 4):
                x_ld[b] = dma(ROW[:, 4 * b:4 * b + 4, 128:256], x_v[:, 4 * b:4 * b + 4, :], sig=f"ld_x{b}")
            do("gpsimd", lambda e: e.memset(ones[:, :], 1.0), sig="cst")
            k["tri"] = do("gpsimd", lambda e: e.affine_select(out=tri[:, :], in_=ones[:, :], compare_op=ALU.is_gt, fill=0.0, base=0,
                                                              pattern=[[1, 128]], channel_multiplier=-1), [q.last("cst")], "cst")
            k["g"] = dma(WG[:, :], a["Wg"], sig="ld_g")
            dma(CS[:, :, :, :], a["cs"], sig="ld_c")
            dma(c8[:, :], a["c8"], sig="ld_c")
            dma(e4[:, :], a["e4"], sig="ld_c")
            k["c"] = dma(tio[:, :], a["tio"], sig="ld_c")
            for i, n in enumerate(("lq1", "lk1", "lq2", "lk2")):
                k["l"] = dma(lam[:, i, :], a[n].rearrange("(a n) -> a n", a=1).broadcast_to([128, 8]), sig="ld_lam")
            k["pad"] = [dma(xs[i][NE * REG:NE * REG + 128, :], pad[:, :], [k_z], f"pad{i}") for i in range(len(SEGS))]
            return k

        def bias(name):
            o, length = BIAS[name]
            return BS[:, o:o + length]

        def lambdas():
            w = do("vector", lambda e: e.tensor_tensor(lam[:, 0:3:2, :], lam[:, 0:3:2, :], lam[:, 1:4:2, :], ALU.mult), [late["l"]], "lam", n=16)
            w = do("vector", lambda e: e.tensor_reduce(lm[:, 0:2], lam[:, 0:3:2, :], AX, ALU.add), [w], "lam", n=16)
            w = do("scalar", lambda e: e.activation(lm[:, 2:4], lm[:, 0:2], ACT.Exp), [w], "lamx", n=2)
            w = do("vector", lambda e: e.tensor_tensor(lm[:, 4:5], lm[:, 3:4], lm[:, 2:3], ALU.subtract), [w], "lam", n=2)
            return do("vector", lambda e: e.tensor_scalar(lm[:, 5:6], lm[:, 4:5], -(0.8 - 0.6 * float(np.exp(-0.3 * 0))), None, ALU.add),
                      [w], "lam", n=2)

        sring = Ring([0, 1, 2])
        oring = Ring([3])
        rring = Ring([4, 5, 6, 7])

        def first_of(b):
            return 4 * b if b < B else 4 * B + 8 * (b - B)

        def batch_of(g):
            return g // 4 if g < 4 * B else B + (g - 4 * B) // 8

        LA = dict(one=True, gpb=4, vw=16, at=8, dv=8, scale=float(1.0 / np.sqrt(40.0)))
        LB = dict(one=False, gpb=8, vw=20, at=16, dv=16, scale=float(8 ** -0.5))

        def kind(b):
            return LA if b < B else LB

        def seg_of(b):
            return [k for k, (lo, hi) in enumerate(SEGS) if lo <= b < hi][0]

        TA = TR[:, :].rearrange("p (u t g w j c) -> p u t g w j c", u=2, t=4, g=4, w=2, j=4)
        TB = TR[:, :].rearrange("p (u v t g w j c) -> p u v t g w j c", u=2, v=2, t=4, g=8, w=2, j=4)[:, :, 0]
        spare = [TR[:, 16384 * u + 8192:16384 * u + 16384].bitcast(F32) for u in range(2)]
        RT = spare[0][:, 0:1536].rearrange("p (z n) -> p z n", z=3)
        OT = spare[0][:, 1536:1792]
        SA = STK[:, :].rearrange("p (g w j n) -> p g w j n", g=4, w=2, j=4)
        SG = STK[:, :].rearrange("p (g x) -> p g x", g=4)[:, :, 0:1024].rearrange("p g (w n) -> p g w n", w=2)
        SKB = STK[:, :].rearrange("p (g x) -> p g x", g=4)[:, :, 2048:4096].rearrange("p g (j n) -> p g j n", j=4)

        def tile_of(b, i):
            return (TA if b < B else TB)[:, b % 2, i]

        hready, indexed, split_done, tp_done = {}, {}, {}, {}
        stack, smax_tok, mrow, st_group, exp_tok, pv_tok, pv_group = {}, {}, {}, {}, {}, {}, {}
        o_use, norm_done, at_read, out_done, scattered, routed, chosen = {}, {}, {}, {}, {}, {}, {}
        seg_done, ld, ld_x, up_done, down_done, sent, weights, fixed = {}, {}, {}, {}, {}, {}, {}, {}
        m_read, mt_read, or_read, hT_read = [None] * 2, [None] * 2, [None] * 2, [None] * 2
        rt_read, rec_read, att_free, gate_free = [None], [None], [None], [None]

        ln_last = [None, None]

        def layernorm(b, z, rank, ready):
            t0 = 4 * (b % 4)
            yield rank, [ready, ln_last[z]]
            for i in range(4):
                w = do("vector", lambda e, i=i: e.bn_stats(st6[:, z, i, :], ROW[:, t0 + i, 128:256]),
                       [ready, ln_last[z]], "lnd")
                if i == 1:
                    yield rank, []
            yield rank, [w]
            for i in range(4):
                w1 = do("vector", lambda e, i=i: e.bn_aggr(mv[:, z, i, :], st6[:, z, i, :]), [w], "lnd", n=8)
            quick = (z == 0 and b < 2) or (z == 1 and b + 1 in [hi for _, hi in SEGS]) or (z == 0 and b == B)
            w = do("gpsimd", lambda e: e.tensor_scalar(vs[:, z, :], mv[:, z, :, 1], EPS, None, ALU.add), [w1, k_cst], "lnp", n=4)
            w = do("gpsimd", lambda e: e.tensor_tensor(rs[:, z, :], vs[:, z, :], half[:, :], ALU.pow), [w], "lnp", n=350)
            if quick:
                yield rank, [w]
            for i in range(4):
                w2 = do("vector" if quick else "gpsimd", lambda e, i=i: e.tensor_scalar(
                    ROW[:, t0 + i, 0:128], ROW[:, t0 + i, 128:256], mv[:, z, i, 0:1], rs[:, z, i:i + 1], ALU.subtract, ALU.mult),
                    [w], "lnd" if quick else "lnp", n=128 if quick else 352)
            ln_last[z] = w2
            return w2

        def gate(b, k, ready, rank):
            t0, z = 4 * (b % 4), b % 2
            hw = yield from layernorm(b, 1, rank, ready)
            ri, bank, free = yield from rring.take(rank, [hw])
            for i in range(4):
                w = do("tensor", lambda e, i=i: e.transpose(ps[:, bank, 128 * i:128 * i + 128], ROW[:, t0 + i, 0:128], idf[:, :]),
                       free + [hw], "g_t" if i == 3 else None, n=256)
            yield rank, [w, att_free[0]]
            wc = do("scalar", lambda e: e.copy(ATT[:, 0, :], ps[:, bank, :]), [w, att_free[0]], "g_c", n=512)
            rring.give(ri, [wc])
            ri, bank2, free = yield from rring.take(rank, [wc])
            o, n = BIAS["bg"]
            do("tensor", lambda e: e.matmul(ps[:, bank2, 0:32], ones3[:, :],
                                            BS[:, o:o + n].rearrange("p (o n) -> p o n", o=1).broadcast_to([128, 4, NE]),
                                            start=True, stop=False, skip_group_check=True), free + [k_bs], n=64)
            for i in range(4):
                w2 = do("tensor", lambda e, i=i: e.matmul(ps[:, bank2, 8 * i:8 * i + 8], ATT[:, 0, 128 * i:128 * i + 128], WG[:, :],
                                                          start=False, stop=(i == 3), skip_group_check=True),
                        [wc, late["g"]], "g_m" if i == 3 else None, n=256)
            att_free[0] = w2
            lg = ps[:, bank2, 0:32].rearrange("p (t n) -> p t n", t=4)
            dd, ex, vv = (G[:, i, :].rearrange("p (t n) -> p t n", t=4) for i in range(3))

            def bc(x):
                return x.rearrange("p (t o) -> p t o", o=1).broadcast_to([128, 4, NE])

            def row(x):
                return x.rearrange("p (o n) -> p o n", o=1).broadcast_to([128, 4, NE])

            def step(*tokens):
                if not (b + 1 == SEGS[k][1] and HOLD[k]):
                    yield rank, list(tokens)

            yield rank, [w2, gate_free[0]]
            w = do("vector", lambda e: e.tensor_reduce(g4[:, 0, :], lg, AX, ALU.max), [w2, gate_free[0]], "gd", n=32)
            yield from step(w)
            vm = do("vector", lambda e: e.tensor_tensor(vv, lg, bc(g4[:, 0, :]), ALU.is_equal), [w], "gd", n=32)
            wd = do("vector", lambda e: e.tensor_tensor(dd, lg, bc(g4[:, 0, :]), ALU.subtract), [w], "gd", n=32)
            rring.give(ri, [wd])
            wx = do("scalar", lambda e: e.activation(ex, dd, ACT.Exp), [wd], "gx", n=32)
            yield from step(vm, late["c"])
            w = do("vector", lambda e: e.tensor_tensor(vv, vv, row(c8[:, :]), ALU.mult), [vm, late["c"]], "gd", n=32)
            yield from step(w)
            w = do("vector", lambda e: e.tensor_reduce(g4[:, 1, :], vv, AX, ALU.max), [w], "gd", n=32)
            oh = OH[:, :, :]
            yield from step(w)
            wo = do("vector", lambda e: e.tensor_tensor(OHb[:, :, :], row(c8[:, :]), bc(g4[:, 1, :]), ALU.is_equal), [w], "gd", n=32)
            woh = do("vector", lambda e: e.tensor_tensor(oh, row(c8[:, :]), bc(g4[:, 1, :]), ALU.is_equal), [w], "gd", n=32)
            ri, bank3, free = yield from rring.take(rank, [wo])
            do("tensor", lambda e: e.matmul(ps[:, bank3, 0:32], tri[:, :], OHb[:, :, :].rearrange("p t n -> p (t n)"),
                                            start=True, stop=False, skip_group_check=True), free + [wo, late["tri"]], n=64)
            for i in range(3):
                do("tensor", lambda e, i=i: e.matmul(ps[:, bank3, 8 * i + 8:32].rearrange("p (t n) -> p t n", n=NE), ones[:, :],
                                                     OHb[:, i:i + 1, :].broadcast_to([128, 3 - i, NE]),
                                                     start=False, stop=(i == 2), skip_group_check=True), [], n=64)
            for i in range(4):
                w = do("tensor", lambda e, i=i: e.matmul(ps[:, bank3, 32:40], ones[:, :], OHb[:, i, :], start=(i == 0), stop=(i == 3)),
                       [], "g_p" if i == 3 else None, n=64)
            if b % 8 == SEGS[k][0] % 8:
                w0 = do("vector", lambda e: e.tensor_copy(OFF[:, z, 0, :], e4[:, :]), [late["c"]], "gd", n=8)
            else:
                w0 = do("vector", lambda e: e.tensor_copy(OFF[:, z, 0, :], OFF[:, 1 - z, 1, :]), [], "gd", n=8)
            ws = do("vector", lambda e: e.tensor_reduce(g4[:, 2, :], ex, AX, ALU.add), [wx], "gd", n=32)
            yield rank, [w]
            w = do("vector", lambda e: e.tensor_tensor(dd, ps[:, bank3, 0:32].rearrange("p (t n) -> p t n", t=4), row(OFF[:, z, 0, :]),
                                                       ALU.add), [w, w0, wx, woh], "gd", n=32)
            wc = do("vector", lambda e: e.tensor_tensor(OFF[:, z, 1, :], OFF[:, z, 0, :], ps[:, bank3, 32:40], ALU.add), [w0], "gd", n=8)
            rring.give(ri, [wc])
            yield from step(w)
            w = do("vector", lambda e: e.tensor_tensor(dd, dd, oh, ALU.mult), [w], "gd", n=32)
            do("vector", lambda e: e.reciprocal(ROW[:, t0:t0 + 4, 256], g4[:, 2, :]), [ws], "gd", n=32)
            wr = do("vector", lambda e: e.tensor_scalar(g4[:, 4, :], g4[:, 2, :], 2.0, None, ALU.mult), [], "gd", n=4)
            yield from step(w)
            w = do("vector", lambda e: e.tensor_reduce(g4[:, 3, :], dd, AX, ALU.add), [w], "gd", n=32)
            wr = do("vector", lambda e: e.reciprocal(ROW[:, t0:t0 + 4, 258], g4[:, 4, :]), [wr], "gd", n=32)
            yield from step(w, scattered.get(b - 4))
            w = do("vector", lambda e: e.tensor_copy(slot[:, t0:t0 + 4], g4[:, 3, :]), [w, scattered.get(b - 4)], "gd", n=4)
            gate_free[0] = w
            for t in range(t0, t0 + 4):
                ws = do("gpsimd", lambda e, t=t: e.indirect_dma_start(
                    out=xs[k][:, :], out_offset=bass.IndirectOffsetOnAxis(ap=slot[:, t:t + 1], axis=0),
                    in_=ROW[:, t, 0:ROWW], in_offset=None), [w, wr, indexed[b]] + ([blanks[0]] if k == len(SEGS) - 1 else []), f"scat{b % 4}", 16, n=380)
            scattered[b] = ws

        def load(b):
            at, rank = b % 4, first_of(b) - 2.5 * kind(b)["gpb"]
            if b >= 4:
                while b - 4 not in scattered or (b >= B and seg_of(b - B) not in seg_done):
                    yield rank, None
                deps = [scattered[b - 4]] + (seg_done[seg_of(b - B)] if b >= B else [])
                yield rank, deps
                src = x_v if b < B else x2_v
                x_ld[b] = dma(ROW[:, 4 * at:4 * at + 4, 128:256], src[:, 4 * (b % B):4 * (b % B) + 4, :], deps, f"ld_x{at}")
            else:
                deps = []
                yield rank, []
            indexed[b] = do("gpsimd", lambda e: e.iota(ROW[:, 4 * at:4 * at + 4, 257].bitcast(I32), pattern=[[128, 4]], base=512 * (b % B),
                                                       channel_multiplier=1), deps, "idx", n=4)

        def ln(b):
            rank = first_of(b) - 2.11 * kind(b)["gpb"]
            while b not in x_ld:
                yield rank, None
            hready[b] = yield from layernorm(b, 0, rank, x_ld[b])

        def columns(b, tfree, vfree):
            Vb = V[:, b % 3, :, :]
            w = None
            if b in (0, 1, 2):
                w = do("vector", lambda e: e.memset(Vb, 0.0), [], "init", n=700)
            if b in (0, 1, 2, B, B + 1, B + 2):
                vw, at = kind(b)["vw"], kind(b)["at"]
                w = do("vector", lambda e: e.memset(Vb[:, :, 0:16 * vw].rearrange("p t (h c) -> p t h c", c=vw)[:, :, :, at], 1.0),
                       vfree + [w], "init", n=64)
            if b in (0, 1):
                w = do("vector", lambda e: e.memset(TA[:, b].rearrange("p t g w j c -> p (t g w j) c")[:, :, 120:128], 0.0), [], "init", n=512)
                for j in range(4):
                    wj = do("vector", lambda e, j=j: e.memset(TA[:, b, :, :, 1, j, 120 + j], 1.0), [w], "init", n=16)
                w = wj
            if b in (B, B + 1):
                w = do("vector", lambda e: e.memset(TB[:, b % 2].rearrange("p t g w j c -> p (t g w j) c")[:, :, 24:32], 0.0), tfree, "init", n=1024)
                w = do("vector", lambda e: e.memset(TB[:, b % 2].rearrange("p t g w j c -> p (t g) w j c")[:, :, 1, :, 24], 1.0), [w], "init", n=128)
            return w

        def second():
            rank = first_of(B) - 10
            yield rank, [late["l"]]
            weights["lam"] = lambdas()
            while (B - 1, 3) not in split_done:
                yield rank, None
            weights["qkv"] = dma(WA[:, 0:768], a["Wqkv"], [hT_read[1]], "ld_wb", n=1200)
            while B - 1 not in out_done:
                yield rank, None
            yield rank, [out_done[B - 1]]
            weights["proj"] = dma(WA[:, 768:1024].rearrange("p (c n) -> p c n", c=2), a["Wproj"], [out_done[B - 1]], "ld_wp")

        def proj(b, i):
            one, gpb, vw, t, hs = kind(b)["one"], kind(b)["gpb"], kind(b)["vw"], 4 * (b % 4) + i, i % 2
            rank = first_of(b) - 3.26 - (4 - i) * gpb / 4 * 1.25
            ring = sring if b == 0 and i % 2 else rring
            vold = first_of(b - 2) - 1
            while b not in hready or (b > 1 and b - 2 not in tp_done) or (b > 2 and vold not in pv_group):
                yield rank, None
            if b not in fixed:
                fixed[b] = columns(b, [tp_done.get(b - 2)], [pv_group.get(vold) if b > 2 else None])
            tfree = [tp_done.get(b - 2), fixed[b]]
            vfree = [pv_group.get(vold) if b > 2 else None, fixed[b]]
            qq, kk = tile_of(b, i)[:, :, 0], tile_of(b, i)[:, :, 1]
            if b >= B:
                while "qkv" not in weights:
                    yield rank, None
            ri, bank, free = yield from ring.take(rank, [hready[b]])
            w = do("tensor", lambda e: e.transpose(ps[:, bank, 0:128], ROW[:, t, 0:128], idf[:, :]), free + [hready[b], k_cst],
                   "ht", n=256)
            yield rank, [w, hT_read[hs]]
            hw = do("scalar", lambda e: e.copy(HT[:, hs, :], ps[:, bank, 0:128]), [w, hT_read[hs]], "htc")
            ring.give(ri, [hw])
            ri, bk, free = yield from ring.take(rank, [hw])
            if one:
                do("tensor", lambda e: e.matmul(ps[:, bk, :], ones3[:, :], bias("br"), start=True, stop=False), free + [k_bs], n=512)
                w = do("tensor", lambda e: e.matmul(ps[:, bk, :], HT[:, hs, :], WA[:, 0:512], start=False, stop=True),
                       [hw, k_w1], "pj", n=2048)
                r = ps[:, bk, :].rearrange("p (g j c) -> p g j c", g=4, j=4)
                r2 = ps[:, bk, :].rearrange("p (g j o c) -> p g j o c", g=4, j=4, o=1).broadcast_to([128, 4, 4, 2, 32])
                yield rank, [w] + tfree
                wh = do("scalar", lambda e: e.copy(qq[:, :, :, 0:64].rearrange("p g j (o c) -> p g j o c", o=2), r2), [w] + tfree,
                        "hi", n=1024)
                ce = "vector" if b == 0 else "gpsimd"
                yield rank, [wh]
                do(ce, lambda e: e.tensor_copy(kk[:, :, :, 0:32], qq[:, :, :, 0:32]), [wh], f"cp{b == 0}", n=700 if b else 140)
                do(ce, lambda e: e.tensor_copy(kk[:, :, :, 64:96], qq[:, :, :, 32:64]), [wh], f"cp{b == 0}", n=700 if b else 140)
                wl = do("vector", lambda e: e.tensor_tensor(qq[:, :, :, 64:96], r, qq[:, :, :, 0:32], ALU.subtract), [wh], "lo", n=512)
                ring.give(ri, [wl])
                wc = do(ce, lambda e: e.tensor_copy(kk[:, :, :, 32:64], qq[:, :, :, 64:96]), [wl], f"cp{b == 0}", n=700 if b else 140)
                ri, bj, free = yield from ring.take(rank)
                do("tensor", lambda e: e.matmul(ps[:, bj, 0:384], ones3[:, :], bias("bqkv"), start=True, stop=False), free, n=384)
                w = do("tensor", lambda e: e.matmul(ps[:, bj, 0:384], HT[:, hs, :], WA[:, 512:896], start=False, stop=True),
                       [], "pj", n=1536)
                hT_read[hs] = w
                qp = ps[:, bj, 0:128]
                kp = ps[:, bj, 128:256]
                vp = ps[:, bj, 256:384].rearrange("p (h c) -> p h c", c=8)

                def heads(x):
                    return x.rearrange("p (g j c) -> p g j c", g=4, j=4)

                def two(x):
                    return x.rearrange("p (g j o c) -> p g j o c", g=4, j=4, o=1).broadcast_to([128, 4, 4, 2, 8])

                k3 = kk[:, :, :, 96:128].rearrange("p g j (o c) -> p g j o c", o=4)[:, :, :, 0:3:2, :]
                yield rank, [w] + vfree
                do("scalar", lambda e: e.copy(qq[:, :, :, 96:112].rearrange("p g j (o c) -> p g j o c", o=2), two(qp)), [w], "hi", n=256)
                do("scalar", lambda e: e.copy(k3, two(kp)), [], "hi", n=256)
                wh = do("scalar", lambda e: e.copy(V[:, b % 3, i, 0:16 * vw].rearrange("p (h c) -> p h c", c=vw)[:, :, 0:8], vp),
                        vfree, "hi")
                yield rank, [wh]
                do("vector", lambda e: e.tensor_tensor(qq[:, :, :, 112:120], heads(qp), qq[:, :, :, 96:104], ALU.subtract), [wh], "lo")
                wl = do("vector", lambda e: e.tensor_tensor(kk[:, :, :, 104:112], heads(kp), kk[:, :, :, 96:104], ALU.subtract), [], "lo")
                ring.give(ri, [wl])
                split_done[b, i] = [wl, wh, wc]
            else:
                w = do("tensor", lambda e: e.matmul(ps[:, bk, :], HT[:, hs, :], WA[:, 0:512], start=True, stop=True),
                       free + [hw, weights["qkv"]], "pj", n=2048)
                pr = ps[:, bk, :].rearrange("p (x c) -> p x c", c=8)

                def tab(z):
                    return CS[:, z, i, :].rearrange("p (o c) -> p o c", o=1).broadcast_to([128, 64, 8])

                yield rank, [w, rt_read[0]]
                do("vector", lambda e: e.tensor_tensor(RT[:, 0, :].rearrange("p (x c) -> p x c", c=8), pr, tab(0), ALU.mult),
                   [w, rt_read[0], late["c"]], "rot", n=512)
                yield rank, []
                wr = do("vector", lambda e: e.tensor_tensor(RT[:, 1, :].rearrange("p (x c) -> p x c", c=8), pr, tab(1), ALU.mult),
                        [], "rot", n=512)
                ring.give(ri, [wr])

                def part(z, h):
                    return RT[:, z, :].rearrange("p (k h c) -> p k h c", k=2, h=2)[:, :, h, :]

                do("gpsimd", lambda e: e.tensor_tensor(part(2, 0), part(0, 0), part(1, 1), ALU.subtract), [wr], "ro2", n=256)
                wf = do("gpsimd", lambda e: e.tensor_tensor(part(2, 1), part(0, 1), part(1, 0), ALU.add), [], "ro2", n=256)
                ri, bj, free = yield from ring.take(rank)
                w = do("tensor", lambda e: e.matmul(ps[:, bj, 0:256], HT[:, hs, :], WA[:, 512:768], start=True, stop=True),
                       free, "pj", n=1024)
                hT_read[hs] = w
                vo = V[:, b % 3, i, 0:16 * vw].rearrange("p (h c) -> p h c", c=vw)[:, :, 0:16].rearrange("p h (o c) -> p h o c", o=2)
                vi = ps[:, bj, 0:256].rearrange("p (o h c) -> p h o c", o=2, c=8)
                yield rank, [w] + vfree
                wv = do("scalar", lambda e: e.copy(vo, vi), [w] + vfree, "hi", n=256)
                ring.give(ri, [wv])
                fq, fk = RT[:, 2, 0:256], RT[:, 2, 256:512]

                def heads(x):
                    return x.rearrange("p (g j c) -> p g j c", g=8, j=4)

                def two(x):
                    return x.rearrange("p (g j o c) -> p g j o c", g=8, j=4, o=1).broadcast_to([128, 8, 4, 2, 8])

                yield rank, [wf] + tfree
                do("scalar", lambda e: e.copy(qq[:, :, :, 0:16].rearrange("p g j (o c) -> p g j o c", o=2), two(fq)), [wf] + tfree,
                   "hi", n=560)
                yield rank, []
                wh = do("scalar", lambda e: e.copy(kk.rearrange("p g j (o c) -> p g j o c", o=4)[:, :, :, 0:3:2, :], two(fk)), [],
                        "hi", n=560)
                do("gpsimd", lambda e: e.tensor_tensor(qq[:, :, :, 16:24], heads(fq), qq[:, :, :, 0:8], ALU.subtract), [wh], "lo", n=256)
                wl = do("gpsimd", lambda e: e.tensor_tensor(kk[:, :, :, 8:16], heads(fk), kk[:, :, :, 0:8], ALU.subtract), [], "lo", n=256)
                rt_read[0] = wl
                split_done[b, i] = [wl, wh, wv]

        def group(g):
            b, sl, rank = batch_of(g), g % 4, g - 3.40
            one, gl = kind(b)["one"], g - first_of(b)
            while g >= 4 and g - 4 not in st_group:
                yield rank, None
            gfree = [st_group.get(g - 4)]
            k_sz = None
            if 4 * B <= g < 4 * B + 4:
                yield rank, gfree
                k_sz = do("vector", lambda e: e.memset(SKB[:, sl].rearrange("p j n -> p (j n)").bitcast(U32), 0), gfree, "sz", n=960)
            out_ = SA[:, sl].rearrange("p w j n -> p (w j) n") if one else SG[:, sl]
            for i in range(4):
                while (b, i) not in split_done:
                    yield rank, None
                yield rank, split_done[b, i] + gfree
                w = do("sync", lambda e, i=i: e.dma_start_transpose(out_[:, :, 128 * i:128 * i + 128],
                                                                    tile_of(b, i)[:, gl].rearrange("p w j c -> p (w j c)")),
                       split_done[b, i] + gfree, f"tp{sl}", 16, n=1244)
            stack[g] = [w]
            if not one:
                yield rank, [w]
                for j in range(4):
                    w3 = dma(SKB[32 * j:32 * j + 32, sl, j, :], SG[32 * j:32 * j + 32, sl, 1, :], [w, k_sz], f"msk{sl}")
                stack[g] = [w, w3]
            if g + 1 == first_of(b + 1):
                tp_done[b] = w

        def smax(g, qt, j):
            sl, c, one = g % 4, 4 * qt + j, g < 4 * B
            while g not in stack or (g >= 2 and g - 2 not in mrow):
                yield g - 2, None
            ri, bank, free = yield from rring.take(g - 1.92 + c / 16, stack[g])
            if one:
                l_, r_ = SA[0:120, sl, 0, j, 128 * qt:128 * qt + 128], SA[0:120, sl, 1, j, :]
            else:
                l_, r_ = SG[:, sl, 0, 128 * qt:128 * qt + 128], SKB[:, sl, j, :]
            w = do("tensor", lambda e: e.matmul(ps[:, bank, :], l_, r_, start=True, stop=True), free + stack[g], "sm", n=512)
            w2 = do("vector", lambda e: e.tensor_reduce(Mb[:, g % 2, 32 * qt + j:32 * qt + j + 1], ps[:, bank, :], AX, ALU.max),
                    [w, m_read[g % 2]], "mx", n=512)
            rring.give(ri, [w2])
            if c == 15:
                smax_tok[g] = (w, w2)

        def mrows(g):
            sl, z, rank, one = g % 4, g % 2, g - 1.03, g < 4 * B
            while g not in smax_tok:
                yield rank, None
            ri, bank, free = yield from rring.take(rank, [smax_tok[g][1]])
            w = do("tensor", lambda e: e.transpose(ps[:, bank, 0:128], Mb[:, z, :], idf[:, :]), free + [smax_tok[g][1]],
                   "mt", n=256)
            m_read[z] = w
            yield rank, [w, mt_read[z]]
            w2 = do("scalar", lambda e: e.mul(Mt[:, z, :], ps[:, bank, 0:128], -1.0), [w, mt_read[z]], "mc")
            rring.give(ri, [w2])
            for qt in range(4):
                src = Mt[32 * qt:32 * qt + 4, z, :]
                if one:
                    dst = SA[120:124, sl, 0, :, 128 * qt:128 * qt + 128]
                    src = src.rearrange("p (o n) -> p o n", o=1).broadcast_to([4, 4, 128])
                else:
                    dst = SG[24:128:32, sl, 0, 128 * qt:128 * qt + 128]
                w3 = dma(dst, src, [w2, smax_tok[g][0]], f"mr{sl}")
            mt_read[z] = w3
            mrow[g] = w3

        def scores(st, j):
            g, kt, sl, z = st // 4, st % 4, st // 4 % 4, st % 3
            L = kind(batch_of(g))
            one = L["one"]
            rank = g + kt / 4 + j / 16
            while g not in mrow or (st >= 3 and st - 3 not in pv_tok):
                yield rank, None
            si, bank, free = yield from sring.take(rank, [mrow[g]])
            if one:
                l_, r_ = SA[0:124, sl, 1, j, 128 * kt:128 * kt + 128], SA[0:124, sl, 0, j, :]
            else:
                l_, r_ = SKB[:, sl, j, 128 * kt:128 * kt + 128], SG[:, sl, 0, :]
            w = do("tensor", lambda e: e.matmul(ps[:, bank, :], l_, r_, start=True, stop=True), free + [mrow[g]], "st", n=512)
            w2 = do("scalar", lambda e: e.activation(P[:, z, j, :], ps[:, bank, :], ACT.Exp, scale=L["scale"]),
                    [w, pv_tok.get(st - 3)], "exp", n=512)
            sring.give(si, [w2])
            if j == 3:
                exp_tok[st] = w2
                if kt == 3:
                    st_group[g] = w

        def pv(st):
            g, kt = st // 4, st % 4
            b, hh, rank = batch_of(g), g % 4, st / 4 + 0.85
            vw = kind(b)["vw"]
            while st not in exp_tok:
                yield rank, None
            if kt == 0:
                o_use[g] = yield from oring.take(rank, [exp_tok[st]])
            else:
                yield rank, [exp_tok[st]]
            oi, bank, free = o_use[g]
            for j in range(4):
                h = 4 * hh + j
                w = do("tensor", lambda e, j=j, h=h: e.matmul(ps[32 * j:32 * j + 32, bank, :], V[:, b % 3, kt, vw * h:vw * h + 32],
                                                              P[:, st % 3, j, :], start=(kt == 0), stop=(kt == 3)),
                       (free if kt == 0 else []) + [exp_tok[st]] + split_done[b, 3], "pv" if j == 3 else None, n=541)
            pv_tok[st] = w
            if kt == 3:
                pv_group[g] = w

        def norm(g):
            z, b, hh, rank = g % 2, batch_of(g), g % 4, g + 0.83
            gl, dv, at = g - first_of(b), kind(b)["dv"], kind(b)["at"]
            while g not in pv_group:
                yield rank, None
            yield rank, [pv_group[g], or_read[0]]
            oi, bank, _ = o_use[g]
            w = do("scalar", lambda e: e.copy(OR[:, :], ps[:, bank, :]), [pv_group[g], or_read[0]], "oc", n=512)
            oring.give(oi, [w])
            rank = g + 1.27
            while b and b - 1 not in at_read:
                yield rank, None
            ri, rb, free = yield from rring.take(rank, [w])
            for i in range(4):
                w1 = do("tensor", lambda e, i=i: e.transpose(ps[:, rb, 128 * i:128 * i + 128], OR[:, 128 * i:128 * i + 128], idf[:, :]),
                        free + [w], "ot" if i == 3 else None, n=256)
            or_read[0] = w1
            o4 = ps[:, rb, :].rearrange("p (t j c) -> p t j c", t=4, j=4)
            rc = rec[:, 0, :].rearrange("p (t j) -> p t j", t=4)
            yield rank, [w1]
            w2 = do("vector", lambda e: e.reciprocal(rc, o4[:, :, :, at]), [w1, rec_read[0]], "nm")
            yield rank, [w2]
            c0 = hh * 4 * dv
            ao = AT[:, :, c0:c0 + 4 * dv].rearrange("p t (j c) -> p t j c", j=4)
            if gl < 4:
                rb4 = rec[:, 0, :].rearrange("p (t j o) -> p t j o", t=4, o=1).broadcast_to([128, 4, 4, dv])
                w3 = do("vector", lambda e: e.tensor_tensor(ao, o4[:, :, :, 0:dv], rb4, ALU.mult), [w2, at_read.get(b - 1)],
                        "nm", n=16 * dv)
                rring.give(ri, [w3])
            else:
                w3 = do("vector", lambda e: e.tensor_scalar(rec[:, 1, :], rec[:, 0, :], lm[:, 5:6], None, ALU.mult),
                        [w2, weights["lam"]], "nm", n=16)
                yield rank, [w3]
                rb4 = rec[:, 1, :].rearrange("p (t j o) -> p t j o", t=4, o=1).broadcast_to([128, 4, 4, dv])
                tmp = OT[:, :].rearrange("p (t j c) -> p t j c", t=4, j=4)
                w3 = do("vector", lambda e: e.tensor_tensor(tmp, o4[:, :, :, 0:dv], rb4, ALU.mult), [w3], "nm", n=256)
                rring.give(ri, [w3])
                yield rank, [w3]
                w3 = do("vector", lambda e: e.tensor_tensor(ao, ao, tmp, ALU.add), [w3], "nm", n=256)
            rec_read[0] = w3
            norm_done[g] = w3

        def out(b):
            one, rank, k = kind(b)["one"], first_of(b + 1) + 1.73, seg_of(b)
            while first_of(b + 1) - 1 not in norm_done:
                yield rank, None
            nd = norm_done[first_of(b + 1) - 1]
            if not one:
                while "proj" not in weights:
                    yield rank, None
            for c in range(1 if one else 2):
                ri, bank, free = yield from rring.take(rank, [nd])
                for i in range(4):
                    w = do("tensor", lambda e, i=i, c=c, bank=bank: e.transpose(ps[:, bank, 128 * i:128 * i + 128],
                                                                                AT[:, i, 128 * c:128 * c + 128], idf[:, :]),
                           free + [nd], "at" if i == 3 else None, n=256)
                yield rank, [w, att_free[0]]
                w2 = do("scalar", lambda e, c=c, bank=bank: e.copy(ATT[:, c, :], ps[:, bank, :]), [w, att_free[0]], "atc", n=512)
                rring.give(ri, [w2])
            at_read[b] = w
            ri, bank, free = yield from rring.take(rank, [w2])
            if one:
                o, n = BIAS["bo"]
                do("tensor", lambda e: e.matmul(ps[:, bank, :], ones3[:, :],
                                                BS[:, o:o + n].rearrange("p (o n) -> p o n", o=1).broadcast_to([128, 4, 128]),
                                                start=True, stop=False, skip_group_check=True), free, n=512)
                for i in range(4):
                    w = do("tensor", lambda e, i=i: e.matmul(ps[:, bank, 128 * i:128 * i + 128], ATT[:, 0, 128 * i:128 * i + 128],
                                                             WA[:, 896:1024], start=False, stop=(i == 3), skip_group_check=True),
                           [w2], "op" if i == 3 else None, n=512)
            else:
                for i in range(4):
                    for c in range(2):
                        w = do("tensor", lambda e, i=i, c=c: e.matmul(ps[:, bank, 128 * i:128 * i + 128],
                                                                      ATT[:, c, 128 * i:128 * i + 128],
                                                                      WA[:, 768 + 128 * c:896 + 128 * c], start=(c == 0), stop=(c == 1)),
                               free + [w2, weights["proj"]], "op" if i == 3 and c == 1 else None, n=512)
            att_free[0] = out_done[b] = w
            xr = ROW[:, 4 * (b % 4):4 * (b % 4) + 4, 128:256]
            yield rank, [w]
            w = do("vector", lambda e: e.tensor_tensor(xr, xr, ps[:, bank, :].rearrange("p (t n) -> p t n", t=4), ALU.add),
                   [w], "res", n=512)
            rring.give(ri, [w])
            yield from gate(b, k, w, rank + 0.2)
            if b + 1 == SEGS[k][1]:
                yield from route(k, b, rank + 0.2)

        def route(k, b, rank):
            n = 4 * (SEGS[k][1] - SEGS[k][0]) + NE - 1
            if k == len(SEGS) - 1:
                n -= NE
            Cn = OFF[:, b % 2, 1, :]
            w0 = gate_free[0]
            rk, tail = ri[:, k % 2, :], k == len(SEGS) - 1
            old = [ld_x[m] for m in range(len(BLOCKS)) if BLOCKS[m][0] == k - 2][-6:] + [q.last(f"fill{k - 2}")] if k > 1 else []
            yield rank, [w0] + old

            def step(*tokens):
                if not HOLD[k]:
                    yield rank, list(tokens)

            w1 = do("vector", lambda e: e.tensor_scalar(e127[:, :], e4[:, :], -1.0, -1.0 if tail else 127.0, ALU.mult, ALU.add), [late["c"]], "rt", n=8)
            if not tail:
                wp = do("vector", lambda e: e.tensor_copy(rk[:, 2 * FT:2 * FT + NE], Cn), [w0] + old, "rt", n=8)
            if tail:
                w = do("vector", lambda e: e.tensor_tensor(E8[:, 3, :], Cn, e127[:, :], ALU.add), [w0, w1], "rt", n=8)
                yield from step(w)
                w = do("vector", lambda e: e.tensor_scalar(E8i[:, 0, :], E8[:, 3, :], 0.0, None, ALU.max), [w], "rt", n=8)
            else:
                w = do("vector", lambda e: e.tensor_tensor(E8i[:, 0, :], Cn, e127[:, :], ALU.add), [w0, w1], "rt", n=8)
            yield from step(w)
            w = do("vector", lambda e: e.tensor_scalar(E8i[:, 1, :], E8i[:, 0, :], 7, None, ALU.logical_shift_right), [w], "rt", n=8)
            yield from step(w)
            w = do("vector", lambda e: e.tensor_copy(E8[:, 0, :], E8i[:, 1, :]), [w], "rt", n=8)
            yield from step(w)
            wn = do("vector", lambda e: e.tensor_scalar(E8[:, 3, :], E8[:, 0, :], -128.0, float(REG), ALU.mult, ALU.add), [w], "rt", n=8)
            at = 0
            for d in (1, 2, 4):
                to = 1 if at != 1 else 2
                do("vector", lambda e, d=d, at=at, to=to: e.tensor_copy(E8[:, to, 0:d], E8[:, at, 0:d]), [w], "rt", n=8)
                w = do("vector", lambda e, d=d, at=at, to=to: e.tensor_tensor(E8[:, to, d:NE], E8[:, at, d:NE], E8[:, at, 0:NE - d],
                                                                              ALU.add), [w], "rt", n=8)
                at = to
                yield from step(w)
            cm = cmp[:, 0:n, :]
            tb = tio[:, 0:n].rearrange("p (t o) -> p t o", o=1).broadcast_to([128, n, NE])

            def every(x):
                return x.rearrange("p (o n) -> p o n", o=1).broadcast_to([128, n, NE])

            w = do("vector", lambda e: e.tensor_tensor(cm, every(E8[:, at, :]), tb, ALU.is_le), [w], "rt", n=250)
            yield from step(w)
            w1 = do("vector", lambda e: e.tensor_reduce(ef[:, 0, 0:n], cm, AX, ALU.add), [w], "rt", n=250)
            yield from step(w1, wn)
            w2 = do("vector", lambda e: e.tensor_tensor(cm, cm, every(E8[:, 3, :]), ALU.mult), [w1, wn], "rt", n=250)
            w1 = do("vector", lambda e: e.tensor_scalar(ef[:, 1, 0:n], ef[:, 0, 0:n], float(NE - 1), None, ALU.min), [w1], "rt", n=32)
            yield from step(w2)
            w2 = do("vector", lambda e: e.tensor_reduce(ef[:, 2, 0:n], cm, AX, ALU.add), [w2], "rt", n=250)
            we = do("vector", lambda e: e.tensor_scalar(rk[:, FT:FT + n], ef[:, 1, 0:n], 128.0, None, ALU.mult), [w1] + old, "rt", n=32)
            yield from step(w2)
            w2 = do("vector", lambda e: e.scalar_tensor_tensor(out=ef[:, 3, 0:n], in0=tio[:, tail:tail + n], scalar=128.0, in1=ef[:, 2, 0:n],
                                                               op0=ALU.mult, op1=ALU.add), [w2], "rt", n=32)
            yield from step(w2)
            w2 = do("vector", lambda e: e.tensor_scalar(rk[:, 0:n], ef[:, 3, 0:n], float(NE * REG), None, ALU.min), [w2], "rt", n=32)

            chosen[k] = [we]
            rows = [w2, late["pad"][k]] + [scattered[m] for m in range(max(SEGS[k][0], b - 3), b + 1)]
            if tail:
                routed[k] = rows
                return

            for i in range(NE):
                yield rank, [wp]

                def fill(e, i=i):
                    v = e.value_load(rk[0:1, 2 * FT + i:2 * FT + i + 1], min_val=i * REG, max_val=i * REG + 7 * S)
                    return e.dma_start(xs[k][bass.ds(v, 128), :], pad[:, :])

                w_pad = do("gpsimd", fill, [wp, k_z], f"fill{k}", 16, n=400)
            routed[k] = rows + [w_pad]

        def blank():
            k = len(SEGS) - 1
            n = 4 * (SEGS[k][1] - SEGS[k][0])
            for i in range(NE):
                while first_of(B) + 2 + i not in mrow:
                    yield first_of(B) + 2 + i, None
                blanks[0] = dma(xs[k][i * REG:i * REG + 128 * n, :].rearrange("(t p) c -> p t c", p=128),
                                pad[:, :].rearrange("p (o c) -> p o c", o=1).broadcast_to([128, n, ROWW]), [k_z], "blank", n=1600)

        blanks = [None]

        BLOCKS = [(k, t) for k, (lo, hi) in enumerate(SEGS) for t in range(4 * (hi - lo) + NE - 1)]

        def rank_of(m):
            k, t = BLOCKS[m]
            return SEG_RANK[k][0] + SEG_RANK[k][1] * t

        TAIL = [m for m, (k, t) in enumerate(BLOCKS) if k == len(SEGS) - 1]
        assert len(TAIL) == 11

        def place(m):
            k, t = BLOCKS[m]
            if m not in TAIL:
                i = t % 3 if k == 0 else t % 7
                w_ = WE[:, i, :] if i < 3 else spare[0][:, 2048:2048 + WEW] if i == 3 else spare[1][:, WEW * (i - 4):WEW * (i - 3)]
                ow = [o for o in range(m) if BLOCKS[o][0] == k and m - o == (3 if k == 0 else 7)] or \
                     [o for o in range(m) if BLOCKS[o][0] == k - 1][-9:]
                return (w_, X[:, m % 6, :], XT[:, m % 2, :], Z[:, m % 2, :], TH[:, m % 2, :], i, m % 6), (ow, m - 6, m - 2, m - 2)
            old, sk = [TR[:, 16384 * u:16384 * u + 8192].bitcast(F32) for u in range(2)], STK[:, :].bitcast(F32)
            zt = P[:, :, :, :].rearrange("p z j n -> p (z j n)")
            w_ = old[t // 3][:, WEW * (t % 3):WEW * (t % 3 + 1)] if t < 6 else sk[:, WEW * (t - 6):WEW * (t - 5)]
            x0 = 5 * WEW + ROWW * t
            return (w_, sk[:, x0:x0 + ROWW] if t < 7 else old[(t - 7) // 2][:, 3 * WEW + ROWW * (t % 2):3 * WEW + ROWW * (t % 2 + 1)],
                    sk[:, 5 * WEW + 7 * ROWW + 128 * (t % 4):5 * WEW + 7 * ROWW + 128 * (t % 4) + 128],
                    zt[:, 512 * (t % 6):512 * (t % 6) + 512], zt[:, 3072 + 512 * (t % 6):3584 + 512 * (t % 6)],
                    f"t{t}", f"t{t}"), ([], -1, m - 6 if t > 5 else -1, m - 4 if t > 3 else -1)

        def fetch_expert(m):
            k, t = BLOCKS[m]
            rank = rank_of(m) - 1
            (w_, _, _, _, _, iw, _), (ow, _, _, _) = place(m)
            if m in TAIL[:NE]:
                while (NB - 1 not in tp_done) if t < 6 else (NG - 1 not in st_group):
                    yield EARLY, None
                deps = [tp_done[NB - 1] if t < 6 else st_group[NG - 1]]
                yield EARLY, deps
                ld[m] = dma(w_, a["we"][128 * t:128 * t + 128, :], deps, f"ldw{iw}", n=1700)
                return
            while k not in chosen or any(o not in down_done for o in ow) or (t > 2 and m - 3 not in ld_x):
                yield rank, None
            deps = chosen[k] + [down_done[o] for o in ow] + free_of(m)
            yield rank, deps
            at = FT + (t - NE if m in TAIL else t)

            def expert(e):
                v = e.value_load(ri[0:1, k % 2, at:at + 1], min_val=0, max_val=(NE - 1) * 128)
                return e.dma_start(w_, a["we"][bass.ds(v, 128), :])

            ld[m] = do("sync", expert, deps, f"ldw{iw}", 16, n=1700)

        def fetch_rows(m):
            k, t = BLOCKS[m]
            rank = rank_of(m) - 1
            (_, x, _, _, _, _, ix), (_, ox, _, _) = place(m)
            if m in TAIL[:NE]:
                while NB - 1 not in scattered or m not in ld:
                    yield rank, None
                deps = [scattered[NB - 1], blanks[0]] + free_of(m)
                yield rank, deps
                ld_x[m] = dma(x, xs[k][REG * t:REG * t + 128, :], deps, f"ldx{ix}", n=800)
                return
            while k not in routed or m not in ld or (ox >= 0 and ox not in sent):
                yield rank, None
            deps = routed[k] + free_of(m) + [sent.get(ox)]
            yield rank, deps
            at = t - NE if m in TAIL else t

            def rows(e):
                v = e.value_load(ri[0:1, k % 2, at:at + 1], min_val=0, max_val=NE * REG)
                return e.dma_start(x, xs[k][bass.ds(v, 128), :])

            ld_x[m] = do("sync", rows, deps, f"ldx{ix}", 16, n=800)

        def free_of(m):
            if m in TAIL:
                return [st_group[NG - 1], tp_done[NB - 1], pv_tok[4 * NG - 1]]
            return [st_group[4 * B - 1]] if BLOCKS[m][0] else []

        def block(m):
            k, t = BLOCKS[m]
            rank = rank_of(m)
            (w_, x, xt_, z, th, _, ix), (_, _, oz, ox) = place(m)
            dst = x2 if k < 2 else a["out"]
            while m not in ld_x or (ox >= 0 and ox not in up_done):
                yield rank, None
            r1 = sring if 4 * NG - 1 in exp_tok else rring
            i0, bank, free = yield from rring.take(rank, [ld_x[m]])
            w = do("tensor", lambda e: e.transpose(ps[:, bank, 0:128], x[:, 0:128], idf[:, :]), free + [ld_x[m]], "f_t", n=256)
            yield rank, [w, up_done.get(ox)]
            xt = do("vector", lambda e: e.tensor_copy(xt_, ps[:, bank, 0:128]), [w, up_done.get(ox)], "f_d")
            rring.give(i0, [xt])
            while oz >= 0 and oz not in down_done:
                yield rank, None
            i1, bank1, free = yield from r1.take(rank, [xt, ld[m]])
            for c in range(4):
                w = do("tensor", lambda e, c=c: e.matmul(ps[:, bank1, 128 * c:128 * c + 128], w_[:, 128 * c:128 * c + 128], xt_,
                                                         start=True, stop=True), free + [xt, ld[m]], "f_u" if c == 3 else None, n=512)
            up_done[m] = w
            wb = do("vector", lambda e: e.scalar_tensor_tensor(out=x[:, 128:256], in0=w_[:, FH + 4 + 4 * D:WEW], scalar=x[:, 256:257],
                                                               in1=x[:, 128:256], op0=ALU.mult, op1=ALU.add), [ld_x[m], ld[m]], "f_d", n=188)
            yield rank, [w, down_done.get(oz)]
            for c in range(4):
                w = do("scalar", lambda e, c=c: e.activation(z[:, 128 * c:128 * c + 128], ps[:, bank1, 128 * c:128 * c + 128], ACT.Identity,
                                                             bias=w_[:, FH + c:FH + c + 1]), [w, down_done.get(oz)],
                       "f_z" if c == 3 else None, n=236)
            r1.give(i1, [w])
            w = do("scalar", lambda e: e.activation(th, z, ACT.Tanh, scale=0.5), [w], "f_z", n=560)
            yield rank, [w]
            w = do("vector", lambda e: e.scalar_tensor_tensor(out=z, in0=th, scalar=1.0, in1=z, op0=ALU.add, op1=ALU.mult),
                   [w], "f_d", n=512)
            i2, bank2, free = yield from rring.take(rank, [w])
            for c in range(4):
                w = do("tensor", lambda e, c=c, w=w: e.matmul(ps[:, bank2, 0:128], z[:, 128 * c:128 * c + 128],
                                                              w_[:, FH + 4 + D * c:FH + 4 + D * c + D], start=(c == 0), stop=(c == 3)),
                       free + [w], "f_o" if c == 3 else None, n=512)
            down_done[m] = w
            yield rank, [w]
            w = do("vector", lambda e: e.scalar_tensor_tensor(out=x[:, 128:256], in0=ps[:, bank2, 0:128], scalar=x[:, 258:259],
                                                              in1=x[:, 128:256], op0=ALU.mult, op1=ALU.add), [w, wb], "f_d", n=188)
            rring.give(i2, [w])
            sent[m] = do("gpsimd", lambda e: e.indirect_dma_start(
                out=dst[:, :], out_offset=bass.IndirectOffsetOnAxis(ap=x[:, 257:258].bitcast(U32), axis=0),
                in_=x[:, 128:256], in_offset=None, bounds_check=T - 1, oob_is_err=False), [w], f"so{ix}", 16, n=380)
            if m + 1 == len(BLOCKS) or BLOCKS[m + 1][0] != k:
                last = TAIL if m in TAIL else range(m - 5, m + 1)
                for i in last:
                    while i not in sent:
                        yield rank, None
                seg_done[k] = [sent[i] for i in last]

        def lane(i):
            for m in range(i, TAIL[0], 5):
                yield from block(m)

        def tail_lane(i):
            for m in TAIL[i::6]:
                yield from block(m)

        late = later()

        def each(stage, *counts):
            for i in np.ndindex(*counts):
                yield from stage(*i)

        def projections(*tiles):
            for i in tiles:
                yield from proj(0, i)
            if tiles[0] == 0:
                for b in range(1, NB):
                    for i in range(4):
                        yield from proj(b, i)

        q.run([each(scores, 4 * NG, 4), each(pv, 4 * NG), each(smax, NG, 4, 4), each(mrows, NG), each(norm, NG), each(group, NG),
               projections(0, 2), projections(1, 3), each(ln, NB), each(load, NB), each(out, NB), second(), each(fetch_expert, TAIL[0]), each(fetch_rows, TAIL[0]), blank(),
               each(lambda t: fetch_expert(TAIL[t]), len(TAIL)), each(lambda t: fetch_rows(TAIL[t]), len(TAIL))]
              + [lane(i) for i in range(5)] + [tail_lane(i) for i in range(6)])
        do("gpsimd", None, seg_done[2] + seg_done[3])

        block = ctx.enter_context(nc.Block())

        @block.sync
        def _(eng):
            q.play("sync", eng)

        @block.gpsimd
        def _(eng):
            q.play("gpsimd", eng)

        @block.scalar
        def _(eng):
            q.play("scalar", eng)

        @block.vector
        def _(eng):
            q.play("vector", eng)

        @block.tensor
        def _(eng):
            q.play("tensor", eng)


def tables():
    inv = (np.float32(1.0) / np.power(np.float32(10000.0), np.arange(0, 16, 2, dtype=np.float32) / np.float32(16))).astype(np.float32)
    f = (np.arange(S, dtype=np.float32)[:, None] * inv[None, :]).astype(np.float32)
    cs = np.stack([np.cos(f), np.sin(f)]).astype(np.float32)
    cs = np.ascontiguousarray(cs.reshape(2, 4, 128, 8).transpose(2, 0, 1, 3))
    c8 = np.tile(np.arange(NE, 0, -1, dtype=np.float32), (128, 1))
    tio = np.tile(np.arange(FT, dtype=np.float32), (128, 1))
    e4 = np.tile(np.arange(NE, dtype=np.float32) * REG, (128, 1))
    return cs, c8, e4, tio


def kernel(**inputs):
    import concourse.bacc as bacc
    from concourse.bass_utils import run_bass_kernel_spmd

    i = {k: np.asarray(v) for k, v in inputs.items()}
    pa, pb, pf = "L0_attn_a_", "L0_attn_b_", "L0_ffn_"
    cs, c8, e4, tio = tables()
    bias = np.concatenate([i[pa + "br"], i[pa + "bq"], i[pa + "bk"], i[pa + "bv"], i[pa + "bo"], i[pf + "bg"]])
    bias = np.concatenate([bias, np.zeros(BIASW * 128 - bias.shape[0], bias.dtype)])
    we = np.concatenate([i[pf + "W1"], i[pf + "b1"].reshape(NE, 4, 128).transpose(0, 2, 1),
                         i[pf + "W2"].reshape(NE, 4, 128, D).transpose(0, 2, 1, 3).reshape(NE, 128, 4 * D),
                         np.broadcast_to(i[pf + "b2"][:, None, :], (NE, 128, D))], axis=2)
    arrays = {
        "x": i[pa + "x"].reshape(T, D), "Wq": i[pa + "Wq"], "Wk": i[pa + "Wk"], "Wv": i[pa + "Wv"], "Wr": i[pa + "Wr"],
        "Wo": i[pa + "Wo"], "bias": bias, "Wg": i[pf + "Wg"], "we": we.reshape(NE * 128, WEW),
        "Wqkv": i[pb + "W_qkv"].T, "Wproj": i[pb + "W_proj"].T.reshape(2, 128, D).transpose(1, 0, 2),
        "lq1": i[pb + "lambda_q1"], "lk1": i[pb + "lambda_k1"], "lq2": i[pb + "lambda_q2"], "lk2": i[pb + "lambda_k2"],
        "cs": cs, "c8": c8, "e4": e4, "tio": tio,
    }
    arrays = {f"in_{k}": np.ascontiguousarray(v) for k, v in arrays.items()}
    nc = bacc.Bacc("TRN2", target_bir_lowering=False, num_devices=1)
    aps = {k[3:]: nc.dram_tensor(k, v.shape, mybir.dt.from_np(v.dtype), kind="ExternalInput").ap() for k, v in arrays.items()}
    aps["out"] = nc.dram_tensor("out0", (T, D), F32, kind="ExternalOutput").ap()
    build(nc, aps)
    r = run_bass_kernel_spmd(nc, [arrays], core_ids=[0])
    return r.results[0]["out0"].reshape(B, S, D)
```
